# Optimizing a Trainium2 kernel written in Bass

```python
import numpy as np
import jax
import jax.numpy as jnp

def _softmax(x, axis=-1):
    return jax.nn.softmax(x, axis=axis)

def _gelu(x):
    return jax.nn.gelu(x, approximate=True)

def _silu(x):
    return jax.nn.silu(x)

def _sigmoid(x):
    return jax.nn.sigmoid(x)

def _layernorm(x, axis=-1, eps=1e-05):
    m = jnp.mean(x, axis=axis, keepdims=True)
    v = jnp.var(x, axis=axis, keepdims=True)
    return (x - m) / jnp.sqrt(v + eps)

def _scatter_add(tgt, idx, src, axis=0):
    return tgt.at[idx].add(src)

def _segment_sum(src, seg, n):
    return jax.ops.segment_sum(src, seg, n)
kernel_name = 'mk_adj_preln_d2_adj_r2_d6cfcb'

def setup_inputs(seed: int=0):
    np.random.seed(seed)
    _w = jnp.asarray

    def _rec_inputs():
        import jax
        import jax.numpy as jnp
        _gk = jax.random.key(seed)
        x = -0.000125 + 0.9999 * jax.random.normal(jax.random.fold_in(_gk, 1), (128, 128, 128), jnp.float32)
        _a = jax.random.bernoulli(jax.random.fold_in(_gk, 2), 0.03125, (128, 128))
        _a = jnp.logical_or(_a, jnp.swapaxes(_a, -1, -2))
        _a = jnp.logical_or(_a, jnp.eye(128, dtype=bool))
        _af = _a.astype(jnp.float32)
        _af = _af * jax.random.uniform(jax.random.fold_in(_gk, 3), (128, 128), jnp.float32, 0.05, 0.000488281)
        adj = _af
        return (x, adj)
    x, adj = _rec_inputs()

    def _L0_gnn_setup():
        import jax, jax.numpy as jnp
        import numpy as np
        B, T, D, H = (64, 1024, 128, 128)
        MAX_SKIP = 4

        def _lstm_last(Wih, Whh, bih, bhh, xs):
            N, _, Hd = xs.shape
            bias = bih + bhh

            def step(carry, x_t):
                h, c = carry
                g = x_t @ Wih.T + h @ Whh.T + bias
                i, f, gg, o = jnp.split(g, 4, axis=-1)
                c = jax.nn.sigmoid(f) * c + jax.nn.sigmoid(i) * jnp.tanh(gg)
                h = jax.nn.sigmoid(o) * jnp.tanh(c)
                return ((h, c), None)
            init = (jnp.zeros((N, Hd), xs.dtype), jnp.zeros((N, Hd), xs.dtype))
            (h_last, _), _ = jax.lax.scan(step, init, jnp.swapaxes(xs, 0, 1))
            return h_last
        key = jax.random.key(seed)
        ks = jax.random.split(key, 8)
        s = 0.05
        x = jax.random.normal(ks[0], (B, T, D), jnp.float32)
        adj = jax.random.uniform(ks[1], (T, T), jnp.float32) / T
        Wg0 = jax.random.normal(ks[2], (D, H), jnp.float32) * s
        bg0 = jnp.zeros((H,), jnp.float32)
        Wg1 = jax.random.normal(ks[3], (H, H), jnp.float32) * s
        bg1 = jnp.zeros((H,), jnp.float32)
        Wih = jax.random.normal(ks[4], (MAX_SKIP, 4 * H, H), jnp.float32) * s
        Whh = jax.random.normal(ks[5], (MAX_SKIP, 4 * H, H), jnp.float32) * s
        bih = jax.random.normal(ks[6], (MAX_SKIP, 4 * H), jnp.float32) * s
        bhh = jax.random.normal(ks[7], (MAX_SKIP, 4 * H), jnp.float32) * s
        return dict(x=x, adj=adj, Wg0=Wg0, bg0=bg0, Wg1=Wg1, bg1=bg1, Wih=Wih, Whh=Whh, bih=bih, bhh=bhh)
    _L0_gnn_all = _L0_gnn_setup()
    _L0_gnn_in = {k: v for k, v in _L0_gnn_all.items() if k in ('Wg0', 'bg0', 'Wg1', 'bg1', 'Wih', 'Whh', 'bih', 'bhh')}
    del _L0_gnn_all

    def _L1_gnn_setup():
        import jax, jax.numpy as jnp
        import numpy as np
        ALPHA = 0.2
        key = jax.random.key(seed)
        k1, k2, k3, k4 = jax.random.split(key, 4)
        B, N, Fin, Fout = (8, 1024, 128, 128)
        h = jax.random.normal(k1, (B, N, Fin), dtype=jnp.float32)
        adj = jax.random.randint(k2, (N, N), 0, 2).astype(jnp.float32)
        adj = jnp.maximum(adj, jnp.eye(N, dtype=jnp.float32))

        def xavier(k, shape, gain=1.414):
            fan_in, fan_out = (shape[0], shape[1])
            a = gain * np.sqrt(6.0 / (fan_in + fan_out))
            return jax.random.uniform(k, shape, dtype=jnp.float32, minval=-a, maxval=a)
        W = xavier(k3, (Fin, Fout))
        a = xavier(k4, (2 * Fout, 1))
        return {'h': h, 'adj_matrix': adj, 'W': W, 'a': a}
    _L1_gnn_all = _L1_gnn_setup()
    _L1_gnn_in = {k: v for k, v in _L1_gnn_all.items() if k in ('W', 'a')}
    del _L1_gnn_all
    return {'x': x, 'adj': adj, 'L0_gnn_Wg0': _L0_gnn_in['Wg0'], 'L0_gnn_bg0': _L0_gnn_in['bg0'], 'L0_gnn_Wg1': _L0_gnn_in['Wg1'], 'L0_gnn_bg1': _L0_gnn_in['bg1'], 'L0_gnn_Wih': _L0_gnn_in['Wih'], 'L0_gnn_Whh': _L0_gnn_in['Whh'], 'L0_gnn_bih': _L0_gnn_in['bih'], 'L0_gnn_bhh': _L0_gnn_in['bhh'], 'L1_gnn_W': _L1_gnn_in['W'], 'L1_gnn_a': _L1_gnn_in['a']}

def reference(x, adj, L0_gnn_Wg0, L0_gnn_bg0, L0_gnn_Wg1, L0_gnn_bg1, L0_gnn_Wih, L0_gnn_Whh, L0_gnn_bih, L0_gnn_bhh, L1_gnn_W, L1_gnn_a):
    import jax
    import jax.numpy as jnp

    def _L0_gnn_ref(x, adj, Wg0, bg0, Wg1, bg1, Wih, Whh, bih, bhh):
        import jax, jax.numpy as jnp
        import numpy as np
        B, T, D, H = (64, 1024, 128, 128)
        MAX_SKIP = 4

        def _lstm_last(Wih, Whh, bih, bhh, xs):
            N, _, Hd = xs.shape
            bias = bih + bhh

            def step(carry, x_t):
                h, c = carry
                g = x_t @ Wih.T + h @ Whh.T + bias
                i, f, gg, o = jnp.split(g, 4, axis=-1)
                c = jax.nn.sigmoid(f) * c + jax.nn.sigmoid(i) * jnp.tanh(gg)
                h = jax.nn.sigmoid(o) * jnp.tanh(c)
                return ((h, c), None)
            init = (jnp.zeros((N, Hd), xs.dtype), jnp.zeros((N, Hd), xs.dtype))
            (h_last, _), _ = jax.lax.scan(step, init, jnp.swapaxes(xs, 0, 1))
            return h_last
        h = jax.nn.relu(jnp.einsum('ts,bsh->bth', adj, x @ Wg0 + bg0))
        h = jax.nn.relu(jnp.einsum('ts,bsh->bth', adj, h @ Wg1 + bg1))
        Bv, Tv, Hd = h.shape
        for p in range(1, MAX_SKIP + 1):
            nw = Tv // p
            wins = h[:, :nw * p, :].reshape(Bv * nw, p, Hd)
            last = _lstm_last(Wih[p - 1], Whh[p - 1], bih[p - 1], bhh[p - 1], wins)
            idx = jnp.arange(nw) * p + (p - 1)
            h = h.at[:, idx, :].set(last.reshape(Bv, nw, Hd))
        return h

    def _L1_gnn_ref(h, adj_matrix, W, a):
        import jax, jax.numpy as jnp
        import numpy as np
        ALPHA = 0.2
        Fout = W.shape[1]
        Wh = jnp.einsum('bnf,fo->bno', h, W)
        a1, a2 = (a[:Fout, 0], a[Fout:, 0])
        s1 = Wh @ a1
        s2 = Wh @ a2
        e = s1[:, :, None] + s2[:, None, :]
        e = jnp.where(e >= 0, e, ALPHA * e)
        e = jnp.where(adj_matrix[None] == 0, -jnp.inf, e)
        attention = jax.nn.softmax(e, axis=-1)
        h_prime = jnp.einsum('bij,bjo->bio', attention, Wh)
        return h_prime
    h = jnp.maximum(_layernorm(x, axis=-1), 0.0)
    x = x + _L0_gnn_ref(h, adj, L0_gnn_Wg0, L0_gnn_bg0, L0_gnn_Wg1, L0_gnn_bg1, L0_gnn_Wih, L0_gnn_Whh, L0_gnn_bih, L0_gnn_bhh)
    h = jnp.maximum(_layernorm(x, axis=-1), 0.0)
    x = x + _L1_gnn_ref(h, adj, L1_gnn_W, L1_gnn_a)
    return x

_drawn_inputs = setup_inputs


def setup_inputs(seed=0):
    import zlib

    import numpy as np

    out = dict(_drawn_inputs(seed))
    spreads = {'L0_gnn_bg0': (0.0, 0.8), 'L0_gnn_bg1': (0.0, 0.8)}
    factors = {'L0_gnn_Wg0': 8.0,
     'L0_gnn_Wg1': 8.0,
     'L0_gnn_Wih': 8.0,
     'L0_gnn_Whh': 8.0,
     'L0_gnn_bih': 2.876,
     'L0_gnn_bhh': 2.872}
    for name, (base, spread) in spreads.items():
        noise = np.random.default_rng([zlib.crc32(name.encode()), seed]).standard_normal(out[name].shape)
        drawn = base * np.exp(spread * noise) if base else spread * noise
        out[name] = jnp.asarray(drawn.astype(out[name].dtype))
    for name, factor in factors.items():
        out[name] = (out[name] * factor).astype(out[name].dtype)
    return out
```

```python
import concourse.bass as bass
from concourse import mybir
from contextlib import ExitStack

fp32 = mybir.dt.float32
fp32r = mybir.dt.float32r
bf16 = mybir.dt.bfloat16
ALU = mybir.AluOpType
ACT = mybir.ActivationFunctionType
AX = mybir.AxisListType

P = 128
BATCHES = 128
EPS = 1e-5
ALPHA = 0.2
MASKED = -(2.0 ** 100)

STREAMS = 2
GB = 8
ROUNDS = BATCHES // (STREAMS * GB)
COLS = GB * P
BANK = 512
NBANK = 4
BB = BANK // P
GATES = 4
I, F, G, O = range(GATES)
MAX_SKIP = 4

STEPS = [(1, 0, 0), (1, 0, 1)] + [(p, k, None) for p in range(2, MAX_SKIP + 1) for k in range(p)]
NSTEP = len(STEPS)


def gates_of(step):
    return (I, G, O) if STEPS[step][1] == 0 else (I, G, F, O)


def width_of(step):
    p, _, half = STEPS[step]
    return GB // 2 * P if half is not None else GB * (P // p)


def _blocks():
    first, emptied_by = {}, []
    for stage, n, engine in (("U0", 2, "act"), ("H1", 2, "act"), ("M1", 2, "dve"), ("H2", 2, "dve")):
        first[stage] = len(emptied_by)
        emptied_by += [engine] * n
    for step in range(NSTEP):
        first[step] = len(emptied_by)
        emptied_by += ["act"] * len(gates_of(step))
    first["T"] = len(emptied_by)
    emptied_by += ["dve"] * 2
    return first, emptied_by


FIRST, EMPTIED_BY = _blocks()
NBLOCK = len(EMPTIED_BY)
ACT_BY = [EMPTIED_BY[:n + 1].count("act") for n in range(NBLOCK)]
DVE_BY = [EMPTIED_BY[:n + 1].count("dve") for n in range(NBLOCK)]
ACT_ALL, DVE_ALL = ACT_BY[-1], DVE_BY[-1]
FORGETS = [sum(STEPS[s][1] > 0 for s in range(n + 1)) for n in range(NSTEP)]
NFORGET = FORGETS[-1]

WX = P + 2
TRIPLES = [(0, 3), (3, 6), (6, 8)]
GAT_BLOCKS = {"T2": (0, 2), "WH": (2, 3), "S2": (5, 2), "PT": (7, 2), "OUT": (9, 3)}
GAT_NBLOCK = 12


def build(nc, x, adj, adjT, Wg0, bg0, Wg1, bg1, WihT, WhhT, bih, bhh, W, WT, a, out):
    ctx = ExitStack()
    with ctx:
        def sb(name, shape, dt=fp32):
            return ctx.enter_context(nc.sbuf_tensor(name, shape, dt))

        def sem(name):
            return ctx.enter_context(nc.semaphore(name))

        XM = sb("XM", [P, BATCHES * P])
        W_x_hi, W_x_lo, W_h_hi, W_h_lo = (sb(n, [P, MAX_SKIP * GATES * P], fp32r)
                                          for n in ("W_x_hi", "W_x_lo", "W_h_hi", "W_h_lo"))
        adjT_sb = sb("adjT_sb", [P, P])
        adj_sb = sb("adj_sb", [P, P])
        Wg0_sb = sb("Wg0_sb", [P, P])
        Wg1_sb = sb("Wg1_sb", [P, P])
        bg1_bc = sb("bg1_bc", [P, P])
        bias_ih = sb("bias_ih", [P, MAX_SKIP * GATES])
        bias_hh = sb("bias_hh", [P, MAX_SKIP * GATES])
        bias = sb("bias", [P, MAX_SKIP * GATES])
        ones = sb("ones", [P, P])
        ident = sb("ident", [P, P])
        ident16 = sb("ident16", [P, P], bf16)
        mask16 = sb("mask16", [P, P], bf16)
        W_ext = sb("W_ext", [P, WX])
        Wa2_bc = sb("Wa2_bc", [P, P])
        WT_sb = sb("WT_sb", [P, P])
        a_sb = sb("a_sb", [P, 2])
        neg_half = sb("neg_half", [P, GB])
        pick_hi = sb("pick_hi", [4, 2])
        pick_lo = sb("pick_lo", [4, 2])
        b0_raw = sb("b0_raw", [4, P])
        b0_parts = sb("b0_parts", [4, 2 * P], fp32r)
        b0_rows = sb("b0_rows", [4, P], fp32r)
        r_raw = sb("r_raw", [4, BANK])
        r_parts = sb("r_parts", [4, 2 * BANK], fp32r)
        r_rows = sb("r_rows", [4, BANK], fp32r)
        tmp_rows = sb("tmp_rows", [4, BANK])

        class Stream:
            pass

        streams = []
        for s in range(STREAMS):
            S = Stream()
            S.s = s
            c = "ab"[s]
            S.hn = sb("hn_" + c, [P, COLS])
            S.h1 = S.hn
            S.U = sb("U_" + c, [P, COLS])
            S.m1 = S.U
            S.h_hi = sb("h_hi_" + c, [P, COLS], fp32r)
            S.h_lo = sb("h_lo_" + c, [P, COLS], fp32r)
            S.H = sb("H_" + c, [P, COLS])
            S.gate = [sb(f"gates{j}_" + c, [P, GATES, BANK]) for j in range(2)]
            S.cell = [sb(f"cell{j}_" + c, [P, BANK]) for j in range(2)]
            S.t_hi = sb("t_hi_" + c, [P, BANK], fp32r)
            S.t_lo = sb("t_lo_" + c, [P, BANK], fp32r)
            S.stats = sb("stats_" + c, [P, GB, 6])
            S.mv = sb("mv_" + c, [P, GB, 2])
            S.var = sb("var_" + c, [P, GB])
            S.rstd = sb("rstd_" + c, [P, GB])
            S.top = sb("top_" + c, [P, GB])
            S.top2 = sb("top2_" + c, [P, GB])
            S.rsum = sb("rsum_" + c, [P, GB])
            S.ps = [ctx.enter_context(nc.psum_tensor(f"ps{j}_" + c, [P, BANK], fp32)) for j in range(NBANK)]
            S.x_in = sem("x_in_" + c)
            S.mm_done = sem("mm_done_" + c)
            S.act_emptied = sem("act_emptied_" + c)
            S.dve_emptied = sem("dve_emptied_" + c)
            S.h2_hi_ready = sem("h2_hi_ready_" + c)
            S.input_ready = sem("input_ready_" + c)
            S.forget_ready = sem("forget_ready_" + c)
            S.cell_ready = sem("cell_ready_" + c)
            S.tanh_ready = sem("tanh_ready_" + c)
            S.h_whole = sem("h_whole_" + c)
            S.h_hi_ready = sem("h_hi_ready_" + c)
            S.h_split = sem("h_split_" + c)
            S.moments_ready = sem("moments_ready_" + c)
            S.var_ready = sem("var_ready_" + c)
            S.rstd_ready = sem("rstd_ready_" + c)
            S.centred = sem("centred_" + c)
            S.hn_ready = sem("hn_ready_" + c)
            S.top_ready = sem("top_ready_" + c)
            S.leaky_ready = sem("leaky_ready_" + c)
            S.scores_ready = sem("scores_ready_" + c)
            S.exp_ready = sem("exp_ready_" + c)
            S.inverse_ready = sem("inverse_ready_" + c)
            S.x_out = sem("x_out_" + c)
            S.hT = S.U
            S.WhX = S.gate[1][:, :, :].rearrange("p g n -> p (g n)")[:, 0:GB * WX].rearrange("p (b c) -> p b c", c=WX)
            S.prob = S.H
            S.PT = S.gate[0][:, 0:2, :].rearrange("p g n -> p (g n)")
            streams.append(S)
        A, B = streams

        consts_in = sem("consts_in")
        weights_in = [sem(f"weights_in{n}") for n in range(2)]
        fills = sem("fills")
        diag_ready = sem("diag_ready")
        prep_mm = sem("prep_mm")
        small = sem("small")
        ones_ready = sem("ones_ready")

        for S in (A, B):
            S.raw = S.gate[0][:, :, :].rearrange("p g n -> p (g n)")

        CONSTS = 11 * 16

        def cols(S, g, n=COLS, at=0):
            start = (g * STREAMS + S.s) * COLS + at
            if isinstance(start, int):
                return XM[:, start:start + n]
            return XM[:, bass.ds(start, n)]

        def by_batch(ap, b=GB):
            return ap.rearrange("p (b c) -> p b c", b=b)

        def windows(buf, step):
            p, k, half = STEPS[step]
            if half is not None:
                return buf[:, half * BANK:(half + 1) * BANK]
            nw = P // p
            v = by_batch(buf[:, :])[:, :, 0:nw * p].rearrange("q b (w p) -> q b w p", p=p)
            return v[:, :, :, k]

        def tile(ap, step):
            n = width_of(step)
            if STEPS[step][2] is not None:
                return ap[:, 0:n]
            return ap[:, 0:n].rearrange("p (b w) -> p b w", b=GB)

        def bufs(step):
            return step % 2 if step < 2 else 0

        def pe_free(pe, S, g, n):
            if n < NBANK:
                pe.wait_ge(S.act_emptied, 1 + g * ACT_ALL)
                pe.wait_ge(S.dve_emptied, 1 + g * DVE_ALL)
            elif EMPTIED_BY[n - NBANK] == "act":
                pe.wait_ge(S.act_emptied, 1 + g * ACT_ALL + ACT_BY[n - NBANK])
            else:
                pe.wait_ge(S.dve_emptied, 1 + g * DVE_ALL + DVE_BY[n - NBANK])

        def pe_job(pe, S, g, job):
            mm = nc.tensor.matmul
            if job == "U0":
                pe.wait_ge(S.hn_ready, g + 1)
                for j in range(2):
                    n = FIRST["U0"] + j
                    pe_free(pe, S, g, n)
                    for b in range(BB):
                        c = (j * BB + b) * P
                        last = mm(S.ps[n % NBANK][:, b * P:(b + 1) * P], S.hn[:, c:c + P], adjT_sb[:, :],
                                  start=(b == 0), stop=True, skip_group_check=True)
                    last.then_inc(S.mm_done, 1)
            elif job == "H1":
                for j in range(2):
                    n = FIRST["H1"] + j
                    pe_free(pe, S, g, n)
                    pe.wait_ge(S.act_emptied, 1 + g * ACT_ALL + ACT_BY[FIRST["U0"] + j])
                    mm(S.ps[n % NBANK][:, :], Wg0_sb[:, :], S.U[:, j * BANK:(j + 1) * BANK], start=True, stop=False)
                    mm(S.ps[n % NBANK][:, :], b0_rows[:, :], r_rows[:, :], start=False, stop=True)\
                        .then_inc(S.mm_done, 1)
            elif job == "M1":
                for j in range(2):
                    n = FIRST["M1"] + j
                    pe_free(pe, S, g, n)
                    pe.wait_ge(S.act_emptied, 1 + g * ACT_ALL + ACT_BY[FIRST["H1"] + j])
                    for b in range(BB):
                        c = (j * BB + b) * P
                        last = mm(S.ps[n % NBANK][:, b * P:(b + 1) * P], S.h1[:, c:c + P], Wg1_sb[:, :],
                                  start=(b == 0), stop=True, skip_group_check=True)
                    last.then_inc(S.mm_done, 1)
            elif job == "H2":
                for j in range(2):
                    n = FIRST["H2"] + j
                    pe_free(pe, S, g, n)
                    pe.wait_ge(S.dve_emptied, 1 + g * DVE_ALL + DVE_BY[FIRST["M1"] + j])
                    for b in range(BB):
                        c = (j * BB + b) * P
                        last = mm(S.ps[n % NBANK][:, b * P:(b + 1) * P], S.m1[:, c:c + P], adjT_sb[:, :],
                                  start=(b == 0), stop=True, skip_group_check=True)
                    last.then_inc(S.mm_done, 1)
            elif job == "T":
                pe.wait_ge(S.h_whole, (g + 1) * NSTEP)
                for j in range(2):
                    n = FIRST["T"] + j
                    pe_free(pe, S, g, n)
                    for b in range(BB):
                        c = (j * BB + b) * P
                        last = nc.tensor.transpose(S.ps[n % NBANK][:, b * P:(b + 1) * P], S.H[:, c:c + P], ident[:, :])
                    last.then_inc(S.mm_done, 1)
            else:
                step = job
                p, k, half = STEPS[step]
                n0 = FIRST[step]
                w = width_of(step)
                gates = gates_of(step)
                if half is not None:
                    pe.wait_ge(S.dve_emptied, 1 + g * DVE_ALL + DVE_BY[FIRST["H2"] + half])
                elif k == 0:
                    pe.wait_ge(S.h_split, g * (NSTEP - 1) + step)
                x_hi, x_lo = windows(S.h_hi, step), windows(S.h_lo, step)
                for m, gate in enumerate(gates):
                    n = n0 + m
                    pe_free(pe, S, g, n)
                    ps = tile(S.ps[n % NBANK], step)
                    c = ((p - 1) * GATES + gate) * P
                    mm(ps, W_x_hi[:, c:c + P], x_hi, start=True, stop=False)
                    mm(ps, W_x_hi[:, c:c + P], x_lo, start=False, stop=False)
                    last = mm(ps, W_x_lo[:, c:c + P], x_hi, start=False, stop=(k == 0))
                    if k == 0:
                        last.then_inc(S.mm_done, 1)
                if k:
                    pe.wait_ge(S.h_split, g * (NSTEP - 1) + step)
                    for m, gate in enumerate(gates):
                        ps = tile(S.ps[(n0 + m) % NBANK], step)
                        c = ((p - 1) * GATES + gate) * P
                        h_hi, h_lo = tile(S.t_hi, step), tile(S.t_lo, step)
                        mm(ps, W_h_hi[:, c:c + P], h_hi, start=False, stop=False)
                        mm(ps, W_h_hi[:, c:c + P], h_lo, start=False, stop=False)
                        mm(ps, W_h_lo[:, c:c + P], h_hi, start=False, stop=True).then_inc(S.mm_done, 1)

        def act_job(act, S, g, job):
            done = g * NBLOCK

            def empty(n, out_ap, func, **kw):
                act.wait_ge(S.mm_done, done + n + 1)
                ps = S.ps[n % NBANK][:, :]
                nc.scalar.activation(out_ap, ps, func, **kw).then_inc(S.act_emptied, 1)

            if job == "U0":
                for j in range(2):
                    empty(FIRST["U0"] + j, S.U[:, j * BANK:(j + 1) * BANK], ACT.Copy)
            elif job == "H1":
                for j in range(2):
                    empty(FIRST["H1"] + j, S.h1[:, j * BANK:(j + 1) * BANK], ACT.Relu)
            elif job == "H2":
                for j in range(2):
                    n = FIRST["H2"] + j
                    act.wait_ge(S.mm_done, done + n + 1)
                    nc.scalar.activation(S.h_hi[:, j * BANK:(j + 1) * BANK], S.ps[n % NBANK][:, :], ACT.Relu)\
                        .then_inc(S.h2_hi_ready, 1)
            elif isinstance(job, int):
                step = job
                p, k, half = STEPS[step]
                w = width_of(step)
                gate = S.gate[bufs(step)]
                for m, q in enumerate(gates_of(step)):
                    n = FIRST[step] + m
                    act.wait_ge(S.mm_done, done + n + 1)
                    c = (p - 1) * GATES + q
                    nc.scalar.activation(gate[:, q, 0:w], S.ps[n % NBANK][:, 0:w],
                                         ACT.Tanh if q == G else ACT.Sigmoid,
                                         bias=bias[:, c:c + 1]).then_inc(S.act_emptied, 1)
                act.wait_ge(S.cell_ready, g * NSTEP + step + 1)
                nc.scalar.activation(gate[:, G, 0:w], S.cell[bufs(step)][:, 0:w], ACT.Tanh)\
                    .then_inc(S.tanh_ready, 1)

        def dve_norm(dve, S, g, x_from_dma):
            if x_from_dma:
                dve.wait_ge(S.x_in, (g + 1) * 16)
            for b in range(GB):
                nc.vector.bn_stats(S.stats[:, b, :], cols(S, g, P, b * P))
            dve.drain()
            for b in range(GB):
                last = nc.vector.bn_aggr(S.mv[:, b, :], S.stats[:, b, :])
            last.then_inc(S.moments_ready, 1)
            dve.wait_ge(S.moments_ready, g + 1 + (0 if x_from_dma else ROUNDS))
            nc.vector.tensor_scalar(S.var[:, :], S.mv[:, :, 1], EPS, None, ALU.add).then_inc(S.var_ready, 1)

        def dve_norm_end(dve, S, g, x_from_dma):
            r = 0 if x_from_dma else ROUNDS
            dve.wait_ge(S.centred, g + 1 + r)
            dve.wait_ge(S.rstd_ready, g + 1 + r)
            nc.vector.scalar_tensor_tensor(by_batch(S.hn[:, :]), by_batch(S.hn[:, :]), 0.0,
                                           S.rstd[:, :].unsqueeze(2).to_broadcast([P, GB, P]),
                                           ALU.max, ALU.mult).then_inc(S.hn_ready, 1)

        def dve_job(dve, S, g, job):
            done = g * NBLOCK
            if job == "M1":
                for j in range(2):
                    n = FIRST["M1"] + j
                    dve.wait_ge(S.mm_done, done + n + 1)
                    nc.vector.tensor_tensor(by_batch(S.m1[:, j * BANK:(j + 1) * BANK], BB),
                                            by_batch(S.ps[n % NBANK][:, :], BB),
                                            bg1_bc[:, :].unsqueeze(1).to_broadcast([P, BB, P]), ALU.add)\
                        .then_inc(S.dve_emptied, 1)
            elif job == "H2":
                for j in range(2):
                    n = FIRST["H2"] + j
                    sl = slice(j * BANK, (j + 1) * BANK)
                    dve.wait_ge(S.h2_hi_ready, g * 2 + j + 1)
                    nc.vector.scalar_tensor_tensor(S.h_lo[:, sl], S.ps[n % NBANK][:, :], 0.0,
                                                   S.h_hi[:, sl].bitcast(fp32), ALU.max, ALU.subtract)\
                        .then_inc(S.dve_emptied, 1)
            elif job == "T":
                for j in range(2):
                    n = FIRST["T"] + j
                    dve.wait_ge(S.mm_done, done + n + 1)
                    xs = cols(S, g, BANK, j * BANK)
                    nc.vector.tensor_tensor(xs, xs, S.ps[n % NBANK][:, :], ALU.add).then_inc(S.dve_emptied, 1)
            elif isinstance(job, int):
                step = job
                p, k, half = STEPS[step]
                w = width_of(step)
                gate = S.gate[bufs(step)]
                cell = S.cell[bufs(step)]
                n = FIRST[step]
                final = k == p - 1
                dve.wait_ge(S.act_emptied, 1 + g * ACT_ALL + ACT_BY[n + 1])
                if k == 0:
                    nc.vector.tensor_tensor(cell[:, 0:w], gate[:, I, 0:w], gate[:, G, 0:w], ALU.mult)\
                        .then_inc(S.cell_ready, 1)
                else:
                    nc.vector.tensor_tensor(gate[:, I, 0:w], gate[:, I, 0:w], gate[:, G, 0:w], ALU.mult)\
                        .then_inc(S.input_ready, 1)
                    dve.wait_ge(S.input_ready, g * NFORGET + FORGETS[step])
                    dve.wait_ge(S.forget_ready, g * NFORGET + FORGETS[step])
                    nc.vector.tensor_tensor(cell[:, 0:w], gate[:, I, 0:w], gate[:, F, 0:w], ALU.add)\
                        .then_inc(S.cell_ready, 1)
                dve.wait_ge(S.tanh_ready, g * NSTEP + step + 1)
                o, t = tile(gate[:, O, :], step), tile(gate[:, G, :], step)
                whole = windows(S.H, step) if final else o
                nc.vector.tensor_tensor(whole, o, t, ALU.mult).then_inc(S.h_whole, 1)
                if step == NSTEP - 1:
                    return
                hi = windows(S.h_hi, step) if final else tile(S.t_hi, step)
                lo = windows(S.h_lo, step) if final else tile(S.t_lo, step)
                dve.wait_ge(S.h_whole, g * NSTEP + step + 1)
                nc.vector.tensor_copy(hi, whole).then_inc(S.h_hi_ready, 1)
                dve.wait_ge(S.h_hi_ready, g * (NSTEP - 1) + step + 1)
                nc.vector.tensor_tensor(lo, whole, hi.bitcast(fp32), ALU.subtract).then_inc(S.h_split, 1)

        def pool_norm(pool, S, g, x_from_dma):
            r = 0 if x_from_dma else ROUNDS
            pool.wait_ge(S.moments_ready, g + 1 + r)
            if not x_from_dma and not (isinstance(g, int) and g == 0):
                pool.wait_ge(S.act_emptied, ACT0 + (g - 1) * 7 + 2)
            nc.gpsimd.tensor_tensor(by_batch(S.hn[:, :]), by_batch(cols(S, g)),
                                    S.mv[:, :, 0:1].to_broadcast([P, GB, P]), ALU.subtract).then_inc(S.centred, 1)
            pool.wait_ge(S.var_ready, g + 1 + r)
            nc.gpsimd.tensor_tensor(S.rstd[:, :], S.var[:, :], neg_half[:, :], ALU.pow).then_inc(S.rstd_ready, 1)

        def pool_job(pool, S, g, job):
            if isinstance(job, int) and STEPS[job][1] > 0:
                step = job
                w = width_of(step)
                gate = S.gate[bufs(step)]
                pool.wait_ge(S.act_emptied, 1 + g * ACT_ALL + ACT_BY[FIRST[step] + 2])
                nc.gpsimd.tensor_tensor(gate[:, F, 0:w], gate[:, F, 0:w], S.cell[bufs(step)][:, 0:w], ALU.mult)\
                    .then_inc(S.forget_ready, 1)

        FRONT = ["U0", "H1", "M1", "H2", 0, 1, 2, 3]
        BACK = list(range(4, NSTEP)) + ["T"]
        NORM_AT = 1

        def rounds(eng, job, norm=None, norm_end=None):
            if norm:
                norm(eng, B, 0, True)
                norm_end and norm_end(eng, B, 0, True)
                norm(eng, A, 0, True)
                norm_end and norm_end(eng, A, 0, True)
            for j in FRONT:
                job(eng, B, 0, j)

            def one(g, more):
                for n, (ja, jb) in enumerate(zip(FRONT, BACK)):
                    job(eng, A, g, ja)
                    job(eng, B, g, jb)
                    if more and norm and n == NORM_AT:
                        norm(eng, B, g + 1, True)
                    if more and norm_end and n == NORM_AT + 2:
                        norm_end(eng, B, g + 1, True)
                for n, ja in enumerate(BACK):
                    job(eng, A, g, ja)
                    if more:
                        job(eng, B, g + 1, FRONT[n])
                        if norm and n == NORM_AT:
                            norm(eng, A, g + 1, True)
                        if norm_end and n == NORM_AT + 2:
                            norm_end(eng, A, g + 1, True)

            with eng.Fori(0, ROUNDS - 1) as g:
                one(g, True)
            one(ROUNDS - 1, False)

        MM0, ACT0, DVE0 = ROUNDS * NBLOCK, 1 + ROUNDS * ACT_ALL, 1 + ROUNDS * DVE_ALL
        GA = {"T2": 2, "WH": 5, "PT": 7}
        GD = {"S2": 2, "OUT": 5}

        def gat_free(pe, S, g, n):
            m = n - NBANK
            if m < 0:
                pe.wait_ge(S.act_emptied, ACT0 + g * 7)
                pe.wait_ge(S.dve_emptied, DVE0 + g * 5)
            elif m < 5:
                pe.wait_ge(S.act_emptied, ACT0 + g * 7 + m + 1)
            elif m < 7:
                pe.wait_ge(S.dve_emptied, DVE0 + g * 5 + m - 4)
            else:
                pe.wait_ge(S.act_emptied, ACT0 + g * 7 + m - 1)

        def pe_gat(pe, S, g, stage):
            mm = nc.tensor.matmul
            n0, count = GAT_BLOCKS[stage]
            if stage == "T2":
                pe.wait_ge(S.hn_ready, ROUNDS + g + 1)
            elif stage == "WH" or stage == "S2":
                pe.wait_ge(S.act_emptied, ACT0 + g * 7 + 2)
            elif stage == "PT":
                pe.wait_ge(S.exp_ready, g + 1)
            else:
                pe.wait_ge(S.act_emptied, ACT0 + g * 7 + 7)
            for j in range(count):
                n = n0 + j
                gat_free(pe, S, g, n)
                ps = S.ps[n % NBANK]
                if stage in ("T2", "PT"):
                    src = S.hn if stage == "T2" else S.prob
                    for b in range(BB):
                        c = (j * BB + b) * P
                        last = nc.tensor.transpose(ps[:, b * P:(b + 1) * P], src[:, c:c + P], ident[:, :])
                elif stage == "S2":
                    mm(ps[:, :], Wa2_bc[:, :], S.hT[:, j * BANK:(j + 1) * BANK], start=True, stop=False)
                    last = mm(ps[:, :].rearrange("p (b c) -> p b c", b=BB), ident16[:, :],
                              mask16[:, :].unsqueeze(1).to_broadcast([P, BB, P]), start=False, stop=True)
                else:
                    lo, hi = TRIPLES[j]
                    for b in range(lo, hi):
                        dst = ps[:, (b - lo) * WX:(b - lo + 1) * WX]
                        if stage == "WH":
                            last = mm(dst, S.hT[:, b * P:(b + 1) * P], W_ext[:, :],
                                      start=(b == lo), stop=True, skip_group_check=True)
                        else:
                            last = mm(dst, S.PT[:, b * P:(b + 1) * P], S.WhX[:, b, :],
                                      start=(b == lo), stop=True, skip_group_check=True)
                last.then_inc(S.mm_done, 1)

        def act_gat(act, S, g, stage):
            n0, count = GAT_BLOCKS[stage]
            if stage in ("T2", "PT"):
                dst = S.hT if stage == "T2" else S.PT
                for j in range(count):
                    n = n0 + j
                    act.wait_ge(S.mm_done, MM0 + g * GAT_NBLOCK + n + 1)
                    nc.scalar.activation(dst[:, j * BANK:(j + 1) * BANK], S.ps[n % NBANK][:, :], ACT.Copy)\
                        .then_inc(S.act_emptied, 1)
            elif stage == "WH":
                for j in range(count):
                    n = n0 + j
                    lo, hi = TRIPLES[j]
                    act.wait_ge(S.mm_done, MM0 + g * GAT_NBLOCK + n + 1)
                    src = S.ps[n % NBANK][:, 0:(hi - lo) * WX].rearrange("p (b c) -> p b c", c=WX)
                    nc.scalar.activation(S.WhX[:, lo:hi, 0:P + 1], src[:, :, 0:P + 1], ACT.Copy)\
                        .then_inc(S.act_emptied, 1)
            elif stage == "S2":
                act.wait_ge(S.scores_ready, g + 1)
                nc.scalar.activation(S.prob[:, :], S.prob[:, :], ACT.Exp).then_inc(S.exp_ready, 1)

        def dve_gat(dve, S, g, stage):
            n0, count = GAT_BLOCKS[stage]
            if stage == "S2":
                s1 = S.WhX[:, :, P]
                for j in range(count):
                    n = n0 + j
                    dve.wait_ge(S.mm_done, MM0 + g * GAT_NBLOCK + n + 1)
                    last = nc.vector.reduce_max(S.top[:, j * BB:(j + 1) * BB],
                                                by_batch(S.ps[n % NBANK][:, :], BB), AX.X)
                last.then_inc(S.top_ready, 1)
                dve.wait_ge(S.act_emptied, ACT0 + g * 7 + 5)
                for j in range(count):
                    n = n0 + j
                    nc.vector.tensor_tensor(by_batch(S.prob[:, j * BANK:(j + 1) * BANK], BB),
                                            by_batch(S.ps[n % NBANK][:, :], BB),
                                            S.WhX[:, j * BB:(j + 1) * BB, P:P + 1].to_broadcast([P, BB, P]), ALU.add)\
                        .then_inc(S.dve_emptied, 1)
                dve.wait_ge(S.top_ready, g * 3 + 1)
                nc.vector.tensor_tensor(S.top[:, :], S.top[:, :], s1, ALU.add).then_inc(S.top_ready, 1)
                dve.wait_ge(S.top_ready, g * 3 + 2)
                nc.vector.scalar_tensor_tensor(S.top2[:, :], S.top[:, :], ALPHA, S.top[:, :], ALU.mult, ALU.max)\
                    .then_inc(S.top_ready, 1)
                dve.wait_ge(S.dve_emptied, DVE0 + g * 5 + 2)
                nc.vector.scalar_tensor_tensor(S.prob[:, :], S.prob[:, :], ALPHA, S.prob[:, :], ALU.mult, ALU.max)\
                    .then_inc(S.leaky_ready, 1)
            elif stage == "OUT":
                for j in range(count):
                    n = n0 + j
                    lo, hi = TRIPLES[j]
                    dve.wait_ge(S.mm_done, MM0 + g * GAT_NBLOCK + n + 1)
                    src = S.ps[n % NBANK][:, 0:(hi - lo) * WX].rearrange("p (b c) -> p b c", c=WX)
                    nc.vector.reciprocal(S.rsum[:, lo:hi], src[:, :, P + 1]).then_inc(S.inverse_ready, 1)
                    dve.wait_ge(S.inverse_ready, g * 3 + j + 1)
                    for b in range(lo, hi):
                        xs = cols(S, g, P, b * P)
                        last = nc.vector.scalar_tensor_tensor(xs, src[:, b - lo, 0:P], S.rsum[:, b:b + 1], xs,
                                                              ALU.mult, ALU.add)
                    last.then_inc(S.dve_emptied, 1)

        def pool_gat(pool, S, g, stage):
            if stage == "S2":
                pool.wait_ge(S.leaky_ready, g + 1)
                pool.wait_ge(S.top_ready, g * 3 + 3)
                nc.gpsimd.tensor_tensor(by_batch(S.prob[:, :]), by_batch(S.prob[:, :]),
                                        S.top2[:, :].unsqueeze(2).to_broadcast([P, GB, P]), ALU.subtract)\
                    .then_inc(S.scores_ready, 1)

        GAT_STAGES = ["T2", "WH", "S2", "PT", "OUT"]

        def attention(eng, job, norm=None, norm_end=None):
            if norm:
                for S in (B, A):
                    norm(eng, S, 0, False)
                    norm_end and norm_end(eng, S, 0, False)

            def one(g, more):
                for stage in GAT_STAGES:
                    for S in (B, A):
                        job(eng, S, g, stage)
                        if more and norm and stage == "WH":
                            norm(eng, S, g + 1, False)
                        if more and norm_end and stage == "S2":
                            norm_end(eng, S, g + 1, False)

            with eng.Fori(0, ROUNDS - 1) as g:
                one(g, True)
            one(ROUNDS - 1, False)

        block = ctx.enter_context(nc.Block())

        @block.sync
        def _(sp):
            x_v = x.rearrange("b t d -> t b d")
            out_v = out.rearrange("b t d -> t b d")

            def load_x(S, g):
                if not (isinstance(g, int) and g == 0):
                    sp.wait_ge(S.x_in, g * 16)
                sp.dma_start(by_batch(cols(S, g)), x_v[:, bass.ds((g * STREAMS + S.s) * GB, GB), :])\
                    .then_inc(S.x_in, 16)

            sp.dma_start(adjT_sb[:, :], adjT).then_inc(consts_in, 16)
            load_x(B, 0)
            sp.dma_start(b0_raw[:, :], bg0.unsqueeze(0).to_broadcast([4, P])).then_inc(consts_in, 16)
            sp.dma_start(Wg0_sb[:, :], Wg0).then_inc(consts_in, 16)
            sp.dma_start(Wg1_sb[:, :], Wg1).then_inc(consts_in, 16)
            sp.dma_start(bg1_bc[:, :], bg1.unsqueeze(0).to_broadcast([P, P])).then_inc(consts_in, 16)
            sp.dma_start(bias_ih[:, :], bih).then_inc(consts_in, 16)
            sp.dma_start(bias_hh[:, :], bhh).then_inc(consts_in, 16)
            sp.dma_start(W_ext[:, 0:P], W).then_inc(consts_in, 16)
            sp.dma_start(WT_sb[:, :], WT).then_inc(consts_in, 16)
            sp.dma_start(a_sb[:, :], a).then_inc(consts_in, 16)
            sp.dma_start(adj_sb[:, :], adj).then_inc(consts_in, 16)
            sp.dma_start(A.raw, WihT).then_inc(weights_in[0], 16)
            sp.dma_start(B.raw, WhhT).then_inc(weights_in[1], 16)
            load_x(A, 0)
            with sp.Fori(1, ROUNDS) as g:
                for S in (B, A):
                    load_x(S, g)
            with sp.Fori(0, ROUNDS) as g:
                for S in (B, A):
                    sp.wait_ge(S.dve_emptied, DVE0 + (g + 1) * 5)
                    sp.dma_start(out_v[:, bass.ds((g * STREAMS + S.s) * GB, GB), :], by_batch(cols(S, g)))\
                        .then_inc(S.x_out, 16)
            for S in (B, A):
                sp.wait_ge(S.x_out, 16 * ROUNDS)

        @block.gpsimd
        def _(pool):
            pool.memset(neg_half[:, :], -0.5).then_inc(fills, 1)
            pool.memset(ones[:, :], 1.0).then_inc(fills, 1)
            pool.memset(ident[:, :], 0.0).then_inc(fills, 1)
            pool.memset(W_ext[:, P + 1:WX], 0.0).then_inc(fills, 1)
            pool.memset(pick_hi[:, :], 0.0).then_inc(fills, 1)
            pool.wait_ge(fills, 5)
            pool.affine_select(out=ident[:, :], in_=ident[:, :], compare_op=ALU.not_equal, fill=1.0, base=0,
                               pattern=[[-1, P]], channel_multiplier=1).then_inc(diag_ready, 1)
            pool.affine_select(out=pick_hi[:, 0:1], in_=pick_hi[:, 0:1], compare_op=ALU.is_ge, fill=1.0, base=-2,
                               pattern=[[0, 1]], channel_multiplier=1).then_inc(diag_ready, 1)
            pool.wait_ge(diag_ready, 2)
            pool.affine_select(out=pick_hi[:, 1:2], in_=pick_hi[:, 1:2], compare_op=ALU.not_equal, fill=1.0, base=0,
                               pattern=[[0, 1]], channel_multiplier=1).then_inc(diag_ready, 1)
            pool.wait_ge(diag_ready, 3)
            pool.affine_select(out=pick_hi[:, 1:2], in_=pick_hi[:, 1:2], compare_op=ALU.not_equal, fill=1.0, base=-2,
                               pattern=[[0, 1]], channel_multiplier=1).then_inc(diag_ready, 1)
            rounds(pool, pool_job, norm=pool_norm)
            for S in (B, A):
                pool.wait_ge(S.h_whole, ROUNDS * NSTEP)
                pool.memset(S.WhX[:, :, P + 1:WX], 1.0).then_inc(ones_ready, 1)
            attention(pool, pool_gat, norm=pool_norm)

        @block.scalar
        def _(act):
            for n, (S, hi) in enumerate(((A, W_x_hi), (B, W_h_hi))):
                act.wait_ge(weights_in[n], 16)
                nc.scalar.activation(hi[:, :], S.raw, ACT.Copy).then_inc(S.act_emptied, 1)
            for S in (A, B):
                act.wait_ge(S.dve_emptied, 1)
            rounds(act, act_job)
            attention(act, act_gat)

        @block.vector
        def _(dve):
            links = [0]

            def link(ins):
                links[0] += 1
                ins.then_inc(small, 1)
                dve.wait_ge(small, links[0])

            dve.wait_ge(consts_in, CONSTS)
            dve.wait_ge(diag_ready, 4)
            link(nc.vector.tensor_copy(ident16[:, :], ident[:, :]))
            link(nc.vector.tensor_scalar(mask16[:, :], adj_sb[:, :], 0.0, MASKED, ALU.is_equal, ALU.mult))
            link(nc.vector.tensor_tensor(bias[:, :], bias_ih[:, :], bias_hh[:, :], ALU.add))
            dve.wait_ge(prep_mm, 1)
            link(nc.vector.tensor_copy(r_raw[:, :], A.ps[0][0:4, :]))
            link(nc.vector.tensor_copy(W_ext[:, P:P + 1], A.ps[1][:, 0:1]))
            link(nc.vector.tensor_copy(Wa2_bc[:, :], A.ps[1][:, 1:2].to_broadcast([P, P])))
            link(nc.vector.tensor_scalar(pick_lo[:, :], pick_hi[:, :], -1.0, 1.0, ALU.mult, ALU.add))
            for raw, parts, rows, c, w in ((b0_raw, b0_parts, b0_rows, 0, P), (r_raw, r_parts, r_rows, 1, BANK)):
                link(nc.vector.tensor_copy(parts[:, 0:w], raw[:, :]))
                link(nc.vector.tensor_tensor(parts[:, w:2 * w], raw[:, :], parts[:, 0:w].bitcast(fp32), ALU.subtract))
                link(nc.vector.tensor_scalar(tmp_rows[:, 0:w], parts[:, 0:w].bitcast(fp32), pick_hi[:, c:c + 1], None,
                                             ALU.mult))
                link(nc.vector.scalar_tensor_tensor(rows[:, :], parts[:, w:2 * w].bitcast(fp32), pick_lo[:, c:c + 1],
                                                    tmp_rows[:, 0:w], ALU.mult, ALU.add))
            for S, hi, lo in ((A, W_x_hi, W_x_lo), (B, W_h_hi, W_h_lo)):
                dve.wait_ge(S.act_emptied, 1)
                nc.vector.tensor_tensor(lo[:, :], S.raw, hi[:, :].bitcast(fp32), ALU.subtract)\
                    .then_inc(S.dve_emptied, 1)
            rounds(dve, dve_job, dve_norm, dve_norm_end)
            attention(dve, dve_gat, dve_norm, dve_norm_end)

        @block.tensor
        def _(pe):
            pe.wait_ge(consts_in, CONSTS)
            pe.wait_ge(fills, 5)
            nc.tensor.matmul(A.ps[0][0:4, :].rearrange("p (b c) -> p b c", b=BB), ones[:, 0:4],
                             adjT_sb[:, :].unsqueeze(1).to_broadcast([P, BB, P]), start=True, stop=True)
            nc.tensor.matmul(A.ps[1][:, 0:2], WT_sb[:, :], a_sb[:, :], start=True, stop=True).then_inc(prep_mm, 1)
            for S in (A, B):
                pe.wait_ge(S.dve_emptied, 1)
            pe.wait_ge(diag_ready, 1)
            rounds(pe, pe_job)
            pe.wait_ge(ones_ready, 2)
            attention(pe, pe_gat)


def kernel(**inputs):
    import numpy as np
    import concourse.bacc as bacc
    from concourse.bass_utils import run_bass_kernel_spmd

    def get(name):
        return np.asarray(inputs[name])

    nc = bacc.Bacc("TRN2", target_bir_lowering=False, num_devices=1)
    laid = {
        "x": get("x"),
        "adj": get("adj"), "adjT": get("adj").T,
        "Wg0": get("L0_gnn_Wg0"), "bg0": get("L0_gnn_bg0"),
        "Wg1": get("L0_gnn_Wg1"), "bg1": get("L0_gnn_bg1"),
        "WihT": get("L0_gnn_Wih").transpose(2, 0, 1).reshape(P, -1),
        "WhhT": get("L0_gnn_Whh").transpose(2, 0, 1).reshape(P, -1),
        "bih": get("L0_gnn_bih").reshape(-1, P).T,
        "bhh": get("L0_gnn_bhh").reshape(-1, P).T,
        "W": get("L1_gnn_W"), "WT": get("L1_gnn_W").T,
        "a": get("L1_gnn_a").reshape(2, P).T,
    }
    arrays, args = {}, []
    for name, v in laid.items():
        v = np.ascontiguousarray(v)
        arrays["in_" + name] = v
        args.append(nc.dram_tensor("in_" + name, v.shape, mybir.dt.from_np(v.dtype), kind="ExternalInput").ap())
    args.append(nc.dram_tensor("out_x", (BATCHES, P, P), fp32, kind="ExternalOutput").ap())
    build(nc, *args)
    r = run_bass_kernel_spmd(nc, [arrays], core_ids=[0])
    return r.results[0]["out_x"]
```

```python
import concourse.bass as bass
from concourse import mybir
from contextlib import ExitStack

fp32 = mybir.dt.float32
fp32r = mybir.dt.float32r
bf16 = mybir.dt.bfloat16
ALU = mybir.AluOpType
ACT = mybir.ActivationFunctionType
AX = mybir.AxisListType

P = 128
BATCHES = 128
EPS = 1e-5
ALPHA = 0.2
MASKED = -(2.0 ** 100)

STREAMS = 2
GB = 8
ROUNDS = BATCHES // (STREAMS * GB)
COLS = GB * P
BANK = 512
NBANK = 4
BB = BANK // P
GATES = 4
I, F, G, O = range(GATES)
MAX_SKIP = 4

STEPS = [(1, 0, 0), (1, 0, 1)] + [(p, k, None) for p in range(2, MAX_SKIP + 1) for k in range(p)]
NSTEP = len(STEPS)
FORGETS = [sum(STEPS[s][1] > 0 for s in range(n + 1)) for n in range(NSTEP)]
NFORGET = FORGETS[-1]
WX = P + 2
TRIPLES = [(0, 3), (3, 6), (6, 8)]


def gates_of(step):
    return (I, G, O) if STEPS[step][1] == 0 else (F, I, G, O)


def width_of(step):
    p, _, half = STEPS[step]
    return GB // 2 * P if half is not None else GB * (P // p)


SEQ = """U0 m.0 m.1 H1 M1 m.2 m.3 H2 m.4 m.5 g.0 t.0 g.1 t.1 m.6 g.2 t.2 x.3 m.7 g.3 T2 t.3 g.4 WH t.4 x.5
g.5 n.0 S2 add.0 add.1 t.5 x.6 g.6 leaky.0 t.6 n.1 leaky.1 g.7 t.7 exp x.8 g.8 n.2 n.3 n.4 PT.0
PT.1 t.8 x.9 g.9 out.0 t.9 n.5 n.6 x.10 g.10 out.1 out.2 t.10 n.7 store T""".split()
LSTM, ATT, NEXT = range(3)


def split(item):
    kind, _, number = item.partition(".")
    return kind, int(number) if number else 0


def part_of(item):
    kind = split(item)[0]
    if kind == "n":
        return NEXT
    return ATT if kind in ("m", "T2", "WH", "S2", "add", "leaky", "exp", "PT", "out", "store") else LSTM


class Block:

    def __init__(self, item, j, part, engine, number, emptied, bank):
        self.item, self.j, self.part, self.engine = item, j, part, engine
        self.number, self.emptied, self.bank = number, emptied, bank


def plan_blocks():
    takes = {"U0": (2, "act"), "H1": (2, "act"), "M1": (2, "dve"), "H2": (2, "dve"), "T": (2, "dve"),
             "T2": (2, "act"), "WH": (3, "act"), "S2": (2, "dve"), "PT": (1, "act"), "out": (1, "dve")}
    plan, held = [], None
    for item in SEQ:
        kind, number = split(item)
        if kind in takes:
            count, engine = takes[kind]
        elif kind == "x" or (kind == "g" and STEPS[number][1] == 0):
            count, engine = len(gates_of(number)), "act"
        else:
            held = None if kind == "g" else held
            continue
        assert held is None, "a step's banks are full until its gates are done"
        held = item if kind == "x" else None
        for j in range(count):
            part = part_of(item)
            mine = [b for b in plan if b.part == part]
            plan.append(Block("g" + item[1:] if kind in "xg" else item, j, part, engine, len(mine),
                              sum(b.engine == engine for b in mine) + 1, len(plan) % NBANK))
    return plan


PLAN = plan_blocks()


def blocks(item):
    return [b for b in PLAN if b.item == item]


def total(part, engine=None):
    return sum(b.part == part and engine in (None, b.engine) for b in PLAN)


AHEAD = 24
TURNS = ("ABBBABABBBBAAABABAAABBABBBAABAABBBBBABBBBAABABBABBAABBBBABBABBBAAABAABBABAABABBBAAABBAABABBAAABAAABA"
         "ABAABBABAAABABABAAAAABAABA")


def order():
    mine = {"A": iter([(item, 0) for item in SEQ]),
            "B": iter([(item, 0) for item in SEQ[AHEAD:]] + [(item, 1) for item in SEQ[:AHEAD]])}
    return [(stream, *next(mine[stream])) for stream in TURNS]


ORDER = order()


def build(nc, x, adj, adjT, Wg0, bg0, Wg1, bg1, WihT, WhhT, bih, bhh, W, WT, a, out):
    ctx = ExitStack()
    with ctx:
        def sb(name, shape, dt=fp32):
            return ctx.enter_context(nc.sbuf_tensor(name, shape, dt))

        def sem(name):
            return ctx.enter_context(nc.semaphore(name))

        W_x_hi, W_x_lo, W_h_hi, W_h_lo = (sb(n, [P, MAX_SKIP * GATES * P], fp32r)
                                          for n in ("W_x_hi", "W_x_lo", "W_h_hi", "W_h_lo"))
        adjT_sb = sb("adjT_sb", [P, P])
        adj_sb = sb("adj_sb", [P, P])
        Wg0_sb = sb("Wg0_sb", [P, P])
        Wg1_sb = sb("Wg1_sb", [P, P])
        bg1_bc = sb("bg1_bc", [P, P])
        bias_ih = sb("bias_ih", [P, MAX_SKIP * GATES])
        bias_hh = sb("bias_hh", [P, MAX_SKIP * GATES])
        bias = sb("bias", [P, MAX_SKIP * GATES])
        ones = sb("ones", [P, P])
        ident = sb("ident", [P, P])
        ident16 = sb("ident16", [P, P], bf16)
        mask16 = sb("mask16", [P, P], bf16)
        W_ext = sb("W_ext", [P, WX])
        Wa2_bc = sb("Wa2_bc", [P, P])
        WT_sb = sb("WT_sb", [P, P])
        a_sb = sb("a_sb", [P, 2])
        neg_half = sb("neg_half", [P, GB])
        pick_hi = sb("pick_hi", [4, 2])
        pick_lo = sb("pick_lo", [4, 2])
        b0_raw = sb("b0_raw", [4, P])
        b0_parts = sb("b0_parts", [4, 2 * P], fp32r)
        b0_rows = sb("b0_rows", [4, P], fp32r)
        r_raw = sb("r_raw", [4, BANK])
        r_parts = sb("r_parts", [4, 2 * BANK], fp32r)
        r_rows = sb("r_rows", [4, BANK], fp32r)
        tmp_rows = sb("tmp_rows", [4, BANK])

        class Norm:
            pass

        class Stream:
            pass

        streams = []
        for s in range(STREAMS):
            S = Stream()
            S.s = s
            c = "ab"[s]
            S.x_res = sb("x_res_" + c, [P, COLS])
            S.xm = sb("xm_" + c, [P, COLS])
            S.xo = sb("xo_" + c, [P, COLS])
            S.hn = sb("hn_" + c, [P, COLS])
            S.h1 = S.hn
            S.U = sb("U_" + c, [P, COLS])
            S.m1 = S.U
            S.h_hi = sb("h_hi_" + c, [P, COLS], fp32r)
            S.h_lo = sb("h_lo_" + c, [P, COLS], fp32r)
            S.H = sb("H_" + c, [P, COLS])
            S.gate = [sb(f"gates{j}_" + c, [P, GATES, BANK]) for j in range(2)]
            S.cell = [sb(f"cell{j}_" + c, [P, BANK]) for j in range(2)]
            S.t_hi = sb("t_hi_" + c, [P, BANK], fp32r)
            S.t_lo = sb("t_lo_" + c, [P, BANK], fp32r)
            S.hn2 = sb("hn2_" + c, [P, COLS])
            S.prob = S.hn2
            S.hT = sb("hT_" + c, [P, COLS])
            S.PT = S.hT
            S.WhX = sb("WhX_" + c, [P, GB, WX])
            S.top = sb("top_" + c, [P, GB])
            S.top2 = sb("top2_" + c, [P, GB])
            S.rsum = sb("rsum_" + c, [P, GB])
            S.raw = S.gate[0][:, :, :].rearrange("p g n -> p (g n)")
            S.ps = [ctx.enter_context(nc.psum_tensor(f"ps{j}_" + c, [P, BANK], fp32)) for j in range(NBANK)]
            S.norm = []
            for n, y in enumerate((S.hn, S.hn2)):
                N = Norm()
                N.x = sb(f"x_norm_{c}", [P, COLS]) if n == 0 else S.xm
                N.y = y
                N.stats = sb(f"stats{n}_" + c, [P, GB, 6])
                N.mv = sb(f"mv{n}_" + c, [P, GB, 2])
                N.var = sb(f"var{n}_" + c, [P, GB])
                N.rstd = sb(f"rstd{n}_" + c, [P, GB])
                N.moments_ready = sem(f"moments{n}_ready_" + c)
                N.var_ready = sem(f"var{n}_ready_" + c)
                N.rstd_ready = sem(f"rstd{n}_ready_" + c)
                N.centred = sem(f"centred{n}_" + c)
                N.done = sem(f"norm{n}_done_" + c)
                S.norm.append(N)
            S.x_norm_in = sem("x_norm_in_" + c)
            S.x_res_in = sem("x_res_in_" + c)
            S.x_out = sem("x_out_" + c)
            S.filled = [sem("lstm_filled_" + c), sem("att_filled_" + c)]
            S.emptied = {"act": [sem("lstm_emptied_act_" + c), sem("att_emptied_act_" + c)],
                         "dve": [sem("lstm_emptied_dve_" + c), sem("att_emptied_dve_" + c)]}
            S.h2_hi_ready = sem("h2_hi_ready_" + c)
            S.input_ready = sem("input_ready_" + c)
            S.forget_ready = sem("forget_ready_" + c)
            S.cell_ready = sem("cell_ready_" + c)
            S.tanh_ready = sem("tanh_ready_" + c)
            S.h_whole = sem("h_whole_" + c)
            S.h_hi_ready = sem("h_hi_ready_" + c)
            S.h_split = sem("h_split_" + c)
            S.top_ready = sem("top_ready_" + c)
            S.leaky_ready = sem("leaky_ready_" + c)
            S.scores_ready = sem("scores_ready_" + c)
            S.exp_ready = sem("exp_ready_" + c)
            S.inverse_ready = sem("inverse_ready_" + c)
            streams.append(S)
        A, B = streams

        consts_in = sem("consts_in")
        CONSTS = 11 * 16
        weights_in = [sem(f"weights_in{n}") for n in range(2)]
        fills = sem("fills")
        FILLS = 7
        diag_ready = sem("diag_ready")
        prep_mm = sem("prep_mm")
        prep_step = sem("prep_step")
        PREP_STEPS = 15
        weights_hi = sem("weights_hi")
        weights_split = sem("weights_split")

        def by_batch(ap, b=GB):
            return ap.rearrange("p (b c) -> p b c", b=b)

        def half(ap, j):
            return ap[:, j * BANK:(j + 1) * BANK]

        def windows(buf, step):
            p, k, part = STEPS[step]
            if part is not None:
                return half(buf, part)
            nw = P // p
            v = by_batch(buf[:, :])[:, :, 0:nw * p].rearrange("q b (w p) -> q b w p", p=p)
            return v[:, :, :, k]

        def tile(ap, step):
            n = width_of(step)
            if STEPS[step][2] is not None:
                return ap[:, 0:n]
            return ap[:, 0:n].rearrange("p (b w) -> p b w", b=GB)

        def scratch(step):
            return step % 2 if STEPS[step][0] == 1 else 0

        def filled(q, block):
            return q * total(block.part) + block.number + 1

        def emptied(q, block):
            return 1 + q * total(block.part, block.engine) + block.emptied

        def wait_filled(eng, S, q, block):
            eng.wait_ge(S.filled[block.part], filled(q, block))

        def wait_emptied(eng, S, q, block):
            eng.wait_ge(S.emptied[block.engine][block.part], emptied(q, block))

        def take(pe, S, r, parts, block):
            n = PLAN.index(block)
            for other in PLAN[n - NBANK::-NBANK] if n >= NBANK else []:
                if other.part in parts:
                    wait_emptied(pe, S, r - (other.part == ATT), other)
                    return
            for engine in ("act", "dve"):
                pe.wait_ge(S.emptied[engine][LSTM], 1 + r * total(LSTM, engine))
                if ATT in parts:
                    pe.wait_ge(S.emptied[engine][ATT], 1 + (r - 1) * total(ATT, engine))

        def pe_item(pe, S, r, item, parts):
            mm = nc.tensor.matmul
            kind, k = split(item)
            mine = blocks(item)
            part = part_of(item)
            q = r - 1 if part == ATT else r

            def by_four(block, lhs, rhs):
                take(pe, S, r, parts, block)
                for b in range(BB):
                    c = (block.j * BB + b) * P
                    last = mm(S.ps[block.bank][:, b * P:(b + 1) * P], lhs[:, c:c + P], rhs[:, :],
                              start=(b == 0), stop=True, skip_group_check=True)
                last.then_inc(S.filled[part], 1)

            def transposed(block, src, j):
                take(pe, S, r, parts, block)
                for b in range(BB):
                    c = (j * BB + b) * P
                    last = nc.tensor.transpose(S.ps[block.bank][:, b * P:(b + 1) * P], src[:, c:c + P], ident[:, :])
                last.then_inc(S.filled[part], 1)

            if kind == "U0":
                pe.wait_ge(S.norm[0].done, r + 1)
                for block in mine:
                    by_four(block, S.hn, adjT_sb)
            elif kind == "H1":
                for block, before in zip(mine, blocks("U0")):
                    take(pe, S, r, parts, block)
                    wait_emptied(pe, S, r, before)
                    ps = S.ps[block.bank][:, :]
                    mm(ps, Wg0_sb[:, :], half(S.U, block.j), start=True, stop=False)
                    mm(ps, b0_rows[:, :], r_rows[:, :], start=False, stop=True).then_inc(S.filled[part], 1)
            elif kind == "M1":
                for block, before in zip(mine, blocks("H1")):
                    wait_emptied(pe, S, r, before)
                    by_four(block, S.h1, Wg1_sb)
            elif kind == "H2":
                for block, before in zip(mine, blocks("M1")):
                    wait_emptied(pe, S, r, before)
                    by_four(block, S.m1, adjT_sb)
            elif kind == "T":
                pe.wait_ge(S.h_whole, (r + 1) * NSTEP)
                for block in mine:
                    transposed(block, S.H, block.j)
            elif kind == "x" or (kind == "g" and STEPS[k][1] == 0):
                p, at, part_of_group = STEPS[k]
                x_hi, x_lo = windows(S.h_hi, k), windows(S.h_lo, k)
                for m, (gate, block) in enumerate(zip(gates_of(k), blocks(f"g.{k}"))):
                    take(pe, S, r, parts, block)
                    ps = tile(S.ps[block.bank], k)
                    c = ((p - 1) * GATES + gate) * P
                    if m == 0 and part_of_group is not None:
                        pe.wait_ge(S.h2_hi_ready, r * 2 + part_of_group + 1)
                    elif m == 0 and at == 0:
                        pe.wait_ge(S.h_hi_ready, r * (NSTEP - 1) + k)
                    mm(ps, W_x_hi[:, c:c + P], x_hi, start=True, stop=False)
                    mm(ps, W_x_lo[:, c:c + P], x_hi, start=False, stop=False)
                    if m == 0 and part_of_group is not None:
                        wait_emptied(pe, S, r, blocks("H2")[part_of_group])
                    elif m == 0 and at == 0:
                        pe.wait_ge(S.h_split, r * (NSTEP - 1) + k)
                    last = mm(ps, W_x_hi[:, c:c + P], x_lo, start=False, stop=(at == 0))
                    if at == 0:
                        last.then_inc(S.filled[part], 1)
            elif kind == "g":
                p = STEPS[k][0]
                h_hi, h_lo = tile(S.t_hi, k), tile(S.t_lo, k)
                pe.wait_ge(S.h_hi_ready, r * (NSTEP - 1) + k)
                for m, (gate, block) in enumerate(zip(gates_of(k), mine)):
                    ps = tile(S.ps[block.bank], k)
                    c = ((p - 1) * GATES + gate) * P
                    mm(ps, W_h_hi[:, c:c + P], h_hi, start=False, stop=False)
                    mm(ps, W_h_lo[:, c:c + P], h_hi, start=False, stop=False)
                    if m == 0:
                        pe.wait_ge(S.h_split, r * (NSTEP - 1) + k)
                    mm(ps, W_h_hi[:, c:c + P], h_lo, start=False, stop=True).then_inc(S.filled[part], 1)
            elif kind == "T2":
                pe.wait_ge(S.norm[1].done, q + 1)
                for block in mine:
                    transposed(block, S.hn2, block.j)
            elif kind == "WH":
                wait_emptied(pe, S, q, blocks("T2")[1])
                for block, (lo, hi) in zip(mine, TRIPLES):
                    take(pe, S, r, parts, block)
                    for b in range(lo, hi):
                        last = mm(S.ps[block.bank][:, (b - lo) * WX:(b - lo + 1) * WX], S.hT[:, b * P:(b + 1) * P],
                                  W_ext[:, :], start=(b == lo), stop=True, skip_group_check=True)
                    last.then_inc(S.filled[part], 1)
            elif kind == "S2":
                wait_emptied(pe, S, q, blocks("T2")[1])
                for block in mine:
                    take(pe, S, r, parts, block)
                    ps = S.ps[block.bank]
                    mm(ps[:, :], Wa2_bc[:, :], half(S.hT, block.j), start=True, stop=False)
                    mm(by_batch(ps[:, :], BB), ident16[:, :], mask16[:, :].unsqueeze(1).to_broadcast([P, BB, P]),
                       start=False, stop=True).then_inc(S.filled[part], 1)
            elif kind == "PT":
                pe.wait_ge(S.exp_ready, q + 1)
                transposed(mine[0], S.prob, k)
            elif kind == "out":
                lo, hi = TRIPLES[k]
                wait_emptied(pe, S, q, blocks("PT.1" if hi > BB else "PT.0")[0])
                take(pe, S, r, parts, mine[0])
                for b in range(lo, hi):
                    last = mm(S.ps[mine[0].bank][:, (b - lo) * WX:(b - lo + 1) * WX], S.PT[:, b * P:(b + 1) * P],
                              S.WhX[:, b, :], start=(b == lo), stop=True, skip_group_check=True)
                last.then_inc(S.filled[part], 1)

        def act_item(act, S, r, item, parts):
            kind, k = split(item)
            mine = blocks(item)
            part = part_of(item)
            q = r - 1 if part == ATT else r

            def empty(block, dst, func, **kw):
                wait_filled(act, S, q, block)
                nc.scalar.activation(dst, S.ps[block.bank][:, :], func, **kw).then_inc(S.emptied["act"][part], 1)

            if kind == "U0":
                for block in mine:
                    empty(block, half(S.U, block.j), ACT.Copy)
            elif kind == "H1":
                for block in mine:
                    empty(block, half(S.h1, block.j), ACT.Relu)
            elif kind == "H2":
                for block in mine:
                    wait_filled(act, S, q, block)
                    nc.scalar.activation(half(S.h_hi, block.j), S.ps[block.bank][:, :], ACT.Relu)\
                        .then_inc(S.h2_hi_ready, 1)
            elif kind == "g":
                p, w = STEPS[k][0], width_of(k)
                for gate, block in zip(gates_of(k), mine):
                    wait_filled(act, S, q, block)
                    c = (p - 1) * GATES + gate
                    nc.scalar.activation(S.gate[scratch(k)][:, gate, 0:w], S.ps[block.bank][:, 0:w],
                                         ACT.Tanh if gate == G else ACT.Sigmoid,
                                         bias=bias[:, c:c + 1]).then_inc(S.emptied["act"][part], 1)
            elif kind == "t":
                w = width_of(k)
                act.wait_ge(S.cell_ready, r * NSTEP + k + 1)
                nc.scalar.activation(S.gate[scratch(k)][:, G, 0:w], S.cell[scratch(k)][:, 0:w], ACT.Tanh)\
                    .then_inc(S.tanh_ready, 1)
            elif kind == "T2":
                for block in mine:
                    empty(block, half(S.hT, block.j), ACT.Copy)
            elif kind == "PT":
                empty(mine[0], half(S.PT, k), ACT.Copy)
            elif kind == "WH":
                for block, (lo, hi) in zip(mine, TRIPLES):
                    wait_filled(act, S, q, block)
                    src = S.ps[block.bank][:, 0:(hi - lo) * WX].rearrange("p (b c) -> p b c", c=WX)
                    nc.scalar.activation(S.WhX[:, lo:hi, 0:P + 1], src[:, :, 0:P + 1], ACT.Copy)\
                        .then_inc(S.emptied["act"][part], 1)
            elif kind == "exp":
                act.wait_ge(S.scores_ready, (q + 1) * 2)
                nc.scalar.activation(S.prob[:, :], S.prob[:, :], ACT.Exp).then_inc(S.exp_ready, 1)
            elif kind == "store":
                act.wait_ge(S.emptied["dve"][ATT], 1 + (q + 1) * total(ATT, "dve"))
                act.dma_start(out_v[:, group(S, q), :], by_batch(S.xo[:, :])).then_inc(S.x_out, 16)

        x_v = x.rearrange("b t d -> t b d")
        out_v = out.rearrange("b t d -> t b d")

        def group(S, g):
            return bass.ds((g * STREAMS + S.s) * GB, GB)

        def dve_norm(dve, S, N, g, piece):
            if piece < 4:
                if piece == 0 and N is S.norm[0]:
                    dve.wait_ge(S.x_norm_in, (g + 1) * 16)
                elif piece == 0:
                    dve.wait_ge(S.emptied["dve"][LSTM], 1 + (g + 1) * total(LSTM, "dve"))
                for b in range(2 * piece, 2 * piece + 2):
                    nc.vector.bn_stats(N.stats[:, b, :], N.x[:, b * P:(b + 1) * P])
                if piece == 3:
                    dve.drain()
                    for b in range(GB):
                        last = nc.vector.bn_aggr(N.mv[:, b, :], N.stats[:, b, :])
                    last.then_inc(N.moments_ready, 1)
            elif piece == 4:
                dve.wait_ge(N.moments_ready, g + 1)
                nc.vector.tensor_scalar(N.var[:, :], N.mv[:, :, 1], EPS, None, ALU.add).then_inc(N.var_ready, 1)
            elif piece == 7:
                dve.wait_ge(N.centred, 2 * (g + 1))
                dve.wait_ge(N.rstd_ready, g + 1)
                nc.vector.scalar_tensor_tensor(by_batch(N.y[:, :]), by_batch(N.y[:, :]), 0.0,
                                               N.rstd[:, :].unsqueeze(2).to_broadcast([P, GB, P]),
                                               ALU.max, ALU.mult).then_inc(N.done, 1)

        def dve_item(dve, S, r, item, parts):
            kind, k = split(item)
            mine = blocks(item)
            part = part_of(item)
            q = r - 1 if part == ATT else r
            if kind == "n":
                dve_norm(dve, S, S.norm[0], r + 1, k)
            elif kind == "m":
                dve_norm(dve, S, S.norm[1], q, k)
            elif kind == "M1":
                for block in mine:
                    wait_filled(dve, S, q, block)
                    nc.vector.tensor_tensor(by_batch(half(S.m1, block.j), BB), by_batch(S.ps[block.bank][:, :], BB),
                                            bg1_bc[:, :].unsqueeze(1).to_broadcast([P, BB, P]), ALU.add)\
                        .then_inc(S.emptied["dve"][part], 1)
            elif kind == "H2":
                for block in mine:
                    dve.wait_ge(S.h2_hi_ready, r * 2 + block.j + 1)
                    nc.vector.scalar_tensor_tensor(half(S.h_lo, block.j), S.ps[block.bank][:, :], 0.0,
                                                   half(S.h_hi, block.j).bitcast(fp32), ALU.max, ALU.subtract)\
                        .then_inc(S.emptied["dve"][part], 1)
            elif kind == "T":
                dve.wait_ge(S.x_res_in, (r + 1) * 16)
                for block in mine:
                    wait_filled(dve, S, q, block)
                    nc.vector.tensor_tensor(half(S.xm, block.j), half(S.x_res, block.j), S.ps[block.bank][:, :],
                                            ALU.add).then_inc(S.emptied["dve"][part], 1)
            elif kind == "g":
                w = width_of(k)
                gate, cell = S.gate[scratch(k)], S.cell[scratch(k)]
                wait_emptied(dve, S, q, mine[gates_of(k).index(G)])
                if STEPS[k][1] == 0:
                    nc.vector.tensor_tensor(cell[:, 0:w], gate[:, I, 0:w], gate[:, G, 0:w], ALU.mult)\
                        .then_inc(S.cell_ready, 1)
                else:
                    nc.vector.tensor_tensor(gate[:, I, 0:w], gate[:, I, 0:w], gate[:, G, 0:w], ALU.mult)\
                        .then_inc(S.input_ready, 1)
                    dve.wait_ge(S.input_ready, r * NFORGET + FORGETS[k])
                    dve.wait_ge(S.forget_ready, r * NFORGET + FORGETS[k])
                    nc.vector.tensor_tensor(cell[:, 0:w], gate[:, I, 0:w], gate[:, F, 0:w], ALU.add)\
                        .then_inc(S.cell_ready, 1)
            elif kind == "t":
                gate = S.gate[scratch(k)]
                final = STEPS[k][1] == STEPS[k][0] - 1
                dve.wait_ge(S.tanh_ready, r * NSTEP + k + 1)
                o, t = tile(gate[:, O, :], k), tile(gate[:, G, :], k)
                whole = windows(S.H, k) if final else o
                nc.vector.tensor_tensor(whole, o, t, ALU.mult).then_inc(S.h_whole, 1)
                if k == NSTEP - 1:
                    return
                hi = windows(S.h_hi, k) if final else tile(S.t_hi, k)
                lo = windows(S.h_lo, k) if final else tile(S.t_lo, k)
                dve.wait_ge(S.h_whole, r * NSTEP + k + 1)
                nc.vector.tensor_copy(hi, whole).then_inc(S.h_hi_ready, 1)
                dve.wait_ge(S.h_hi_ready, r * (NSTEP - 1) + k + 1)
                nc.vector.tensor_tensor(lo, whole, hi.bitcast(fp32), ALU.subtract).then_inc(S.h_split, 1)
            elif kind == "S2":
                for block in mine:
                    wait_filled(dve, S, q, block)
                    last = nc.vector.reduce_max(S.top[:, block.j * BB:(block.j + 1) * BB],
                                                by_batch(S.ps[block.bank][:, :], BB), AX.X)
                last.then_inc(S.top_ready, 1)
                dve.wait_ge(S.top_ready, q * 3 + 1)
                wait_emptied(dve, S, q, blocks("WH")[2])
                nc.vector.tensor_tensor(S.top[:, :], S.top[:, :], S.WhX[:, :, P], ALU.add).then_inc(S.top_ready, 1)
                dve.wait_ge(S.top_ready, q * 3 + 2)
                nc.vector.scalar_tensor_tensor(S.top2[:, :], S.top[:, :], ALPHA, S.top[:, :], ALU.mult, ALU.max)\
                    .then_inc(S.top_ready, 1)
            elif kind == "add":
                block = blocks("S2")[k]
                nc.vector.tensor_tensor(by_batch(half(S.prob, k), BB), by_batch(S.ps[block.bank][:, :], BB),
                                        S.WhX[:, k * BB:(k + 1) * BB, P:P + 1].to_broadcast([P, BB, P]), ALU.add)\
                    .then_inc(S.emptied["dve"][part], 1)
            elif kind == "leaky":
                wait_emptied(dve, S, q, blocks("S2")[k])
                s = half(S.prob, k)
                nc.vector.scalar_tensor_tensor(s, s, ALPHA, s, ALU.mult, ALU.max).then_inc(S.leaky_ready, 1)
            elif kind == "out":
                lo, hi = TRIPLES[k]
                wait_filled(dve, S, q, mine[0])
                src = S.ps[mine[0].bank][:, 0:(hi - lo) * WX].rearrange("p (b c) -> p b c", c=WX)
                nc.vector.reciprocal(S.rsum[:, lo:hi], src[:, :, P + 1]).then_inc(S.inverse_ready, 1)
                if k == 0:
                    dve.wait_ge(S.x_out, 1 + q * 16)
                dve.wait_ge(S.inverse_ready, q * 3 + k + 1)
                for b in range(lo, hi):
                    c = slice(b * P, (b + 1) * P)
                    last = nc.vector.scalar_tensor_tensor(S.xo[:, c], src[:, b - lo, 0:P], S.rsum[:, b:b + 1],
                                                          S.xm[:, c], ALU.mult, ALU.add)
                last.then_inc(S.emptied["dve"][part], 1)

        def pool_norm(pool, S, N, g, piece):
            if piece == 4:
                pool.wait_ge(N.var_ready, g + 1)
                nc.gpsimd.tensor_tensor(N.rstd[:, :], N.var[:, :], neg_half[:, :], ALU.pow).then_inc(N.rstd_ready, 1)
            elif piece in (5, 6):
                if piece == 5:
                    pool.wait_ge(N.moments_ready, g + 1)
                j = piece - 5
                nc.gpsimd.tensor_tensor(by_batch(half(N.y, j), BB), by_batch(half(N.x, j), BB),
                                        N.mv[:, j * BB:(j + 1) * BB, 0:1].to_broadcast([P, BB, P]), ALU.subtract)\
                    .then_inc(N.centred, 1)

        def pool_item(pool, S, r, item, parts):
            kind, k = split(item)
            part = part_of(item)
            q = r - 1 if part == ATT else r
            if kind == "n":
                pool_norm(pool, S, S.norm[0], r + 1, k)
            elif kind == "m":
                pool_norm(pool, S, S.norm[1], q, k)
            elif kind == "g" and STEPS[k][1] > 0:
                w = width_of(k)
                forget = S.gate[scratch(k)][:, F, 0:w]
                wait_emptied(pool, S, q, blocks(item)[gates_of(k).index(F)])
                nc.gpsimd.tensor_tensor(forget, forget, S.cell[scratch(k)][:, 0:w], ALU.mult)\
                    .then_inc(S.forget_ready, 1)
            elif kind == "leaky":
                pool.wait_ge(S.leaky_ready, q * 2 + k + 1)
                if k == 0:
                    pool.wait_ge(S.top_ready, q * 3 + 3)
                s = by_batch(half(S.prob, k), BB)
                nc.gpsimd.tensor_tensor(s, s, S.top2[:, k * BB:(k + 1) * BB].unsqueeze(2).to_broadcast([P, BB, P]),
                                        ALU.subtract).then_inc(S.scores_ready, 1)

        def walk(eng, do, constants, weights):
            def parts_of_round(r):
                if not isinstance(r, int):
                    return {LSTM, ATT, NEXT}
                return {p for p, g in ((LSTM, r), (ATT, r - 1), (NEXT, r + 1)) if 0 <= g < ROUNDS}

            def one(r):
                for stream, item, ahead in ORDER:
                    there = parts_of_round(r + ahead)
                    if part_of(item) in there:
                        do(eng, A if stream == "A" else B, r + ahead, item, there)

            for k in range(8):
                do(eng, B, -1, f"n.{k}", {NEXT})
            constants(eng)
            first = [item for stream, item, ahead in ORDER if ahead and part_of(item) != ATT]
            for n, item in enumerate(first):
                if item == "g.0":
                    weights(eng)
                do(eng, B, 0, item, {LSTM, NEXT})
                if n < 8:
                    do(eng, A, -1, f"n.{n}", {NEXT})
            one(0)
            with eng.Fori(1, ROUNDS - 1) as r:
                one(r)
            one(ROUNDS - 1)
            one(ROUNDS)

        block = ctx.enter_context(nc.Block())

        @block.sync
        def _(sp):
            def load_norm(S, g):
                if not (isinstance(g, int) and g == 0):
                    sp.wait_ge(S.norm[0].centred, g * 2)
                sp.dma_start(by_batch(S.norm[0].x[:, :]), x_v[:, group(S, g), :]).then_inc(S.x_norm_in, 16)

            def load_res(S, g):
                if not (isinstance(g, int) and g == 0):
                    sp.wait_ge(S.emptied["dve"][LSTM], 1 + g * total(LSTM, "dve"))
                sp.dma_start(by_batch(S.x_res[:, :]), x_v[:, group(S, g), :]).then_inc(S.x_res_in, 16)

            load_norm(B, 0)
            sp.dma_start(adjT_sb[:, :], adjT).then_inc(consts_in, 16)
            sp.dma_start(b0_raw[:, :], bg0.unsqueeze(0).to_broadcast([4, P])).then_inc(consts_in, 16)
            sp.dma_start(Wg0_sb[:, :], Wg0).then_inc(consts_in, 16)
            sp.dma_start(Wg1_sb[:, :], Wg1).then_inc(consts_in, 16)
            sp.dma_start(bg1_bc[:, :], bg1.unsqueeze(0).to_broadcast([P, P])).then_inc(consts_in, 16)
            sp.dma_start(bias_ih[:, :], bih).then_inc(consts_in, 16)
            sp.dma_start(bias_hh[:, :], bhh).then_inc(consts_in, 16)
            sp.dma_start(W_ext[:, 0:P], W).then_inc(consts_in, 16)
            sp.dma_start(WT_sb[:, :], WT).then_inc(consts_in, 16)
            sp.dma_start(a_sb[:, :], a).then_inc(consts_in, 16)
            sp.dma_start(adj_sb[:, :], adj).then_inc(consts_in, 16)
            load_norm(A, 0)
            sp.dma_start(A.raw, WihT).then_inc(weights_in[0], 16)
            sp.dma_start(B.raw, WhhT).then_inc(weights_in[1], 16)
            for S in (B, A):
                load_res(S, 0)
            with sp.Fori(1, ROUNDS) as g:
                for S in (B, A):
                    load_norm(S, g)
                    load_res(S, g)
            for S in (B, A):
                sp.wait_ge(S.x_out, 1 + 16 * ROUNDS)

        @block.gpsimd
        def _(pool):
            pool.memset(neg_half[:, :], -0.5).then_inc(fills, 1)
            pool.memset(ones[:, :], 1.0).then_inc(fills, 1)
            pool.memset(ident[:, :], 0.0).then_inc(fills, 1)
            pool.memset(W_ext[:, P + 1:WX], 0.0).then_inc(fills, 1)
            for S in (A, B):
                pool.memset(S.WhX[:, :, P + 1:WX], 1.0).then_inc(fills, 1)
            pool.memset(pick_hi[:, :], 0.0).then_inc(fills, 1)
            pool.wait_ge(fills, FILLS)
            pool.affine_select(out=ident[:, :], in_=ident[:, :], compare_op=ALU.not_equal, fill=1.0, base=0,
                               pattern=[[-1, P]], channel_multiplier=1).then_inc(diag_ready, 1)
            pool.affine_select(out=pick_hi[:, 0:1], in_=pick_hi[:, 0:1], compare_op=ALU.is_ge, fill=1.0, base=-2,
                               pattern=[[0, 1]], channel_multiplier=1).then_inc(diag_ready, 1)
            for n, row in enumerate((0, 2)):
                pool.wait_ge(diag_ready, 2 + n)
                pool.affine_select(out=pick_hi[:, 1:2], in_=pick_hi[:, 1:2], compare_op=ALU.not_equal, fill=1.0,
                                   base=-row, pattern=[[0, 1]], channel_multiplier=1).then_inc(diag_ready, 1)
            walk(pool, pool_item, lambda pool: None, lambda pool: None)

        @block.scalar
        def _(act):
            act.wait_ge(fills, FILLS)
            for S in (A, B):
                nc.scalar.activation(S.rsum[:, 2:3], neg_half[:, 0:1], ACT.Copy).then_inc(S.x_out, 1)
                for part in (LSTM, ATT):
                    nc.scalar.activation(S.rsum[:, part:part + 1], neg_half[:, 0:1], ACT.Copy)\
                        .then_inc(S.emptied["act"][part], 1)

            def high_parts(act):
                for n, (S, hi) in enumerate(((A, W_x_hi), (B, W_h_hi))):
                    act.wait_ge(weights_in[n], 16)
                    nc.scalar.activation(hi[:, :], S.raw, ACT.Copy).then_inc(weights_hi, 1)
                act.wait_ge(weights_split, 2)

            walk(act, act_item, lambda act: None, high_parts)

        @block.vector
        def _(dve):
            links = [0]

            def link(ins):
                links[0] += 1
                ins.then_inc(prep_step, 1)
                dve.wait_ge(prep_step, links[0])

            dve.wait_ge(fills, FILLS)
            for S in (A, B):
                for part in (LSTM, ATT):
                    nc.vector.tensor_copy(S.top[:, part:part + 1], neg_half[:, 0:1])\
                        .then_inc(S.emptied["dve"][part], 1)

            def make_constants(dve):
                dve.wait_ge(consts_in, CONSTS)
                dve.wait_ge(diag_ready, 4)
                link(nc.vector.tensor_copy(ident16[:, :], ident[:, :]))
                link(nc.vector.tensor_scalar(mask16[:, :], adj_sb[:, :], 0.0, MASKED, ALU.is_equal, ALU.mult))
                link(nc.vector.tensor_tensor(bias[:, :], bias_ih[:, :], bias_hh[:, :], ALU.add))
                dve.wait_ge(prep_mm, 1)
                link(nc.vector.tensor_copy(r_raw[:, :], A.ps[0][0:4, :]))
                link(nc.vector.tensor_copy(W_ext[:, P:P + 1], A.ps[1][:, 0:1]))
                link(nc.vector.tensor_copy(Wa2_bc[:, :], A.ps[1][:, 1:2].to_broadcast([P, P])))
                link(nc.vector.tensor_scalar(pick_lo[:, :], pick_hi[:, :], -1.0, 1.0, ALU.mult, ALU.add))
                for raw, parts, rows, c, w in ((b0_raw, b0_parts, b0_rows, 0, P), (r_raw, r_parts, r_rows, 1, BANK)):
                    link(nc.vector.tensor_copy(parts[:, 0:w], raw[:, :]))
                    link(nc.vector.tensor_tensor(parts[:, w:2 * w], raw[:, :], parts[:, 0:w].bitcast(fp32), ALU.subtract))
                    link(nc.vector.tensor_scalar(tmp_rows[:, 0:w], parts[:, 0:w].bitcast(fp32), pick_hi[:, c:c + 1], None,
                                                 ALU.mult))
                    link(nc.vector.scalar_tensor_tensor(rows[:, :], parts[:, w:2 * w].bitcast(fp32), pick_lo[:, c:c + 1],
                                                        tmp_rows[:, 0:w], ALU.mult, ALU.add))

            def low_parts(dve):
                for n, (S, hi, lo) in enumerate(((A, W_x_hi, W_x_lo), (B, W_h_hi, W_h_lo))):
                    dve.wait_ge(weights_hi, n + 1)
                    nc.vector.tensor_tensor(lo[:, :], S.raw, hi[:, :].bitcast(fp32), ALU.subtract)\
                        .then_inc(weights_split, 1)

            walk(dve, dve_item, make_constants, low_parts)

        @block.tensor
        def _(pe):
            pe.wait_ge(consts_in, CONSTS)
            pe.wait_ge(fills, FILLS)
            nc.tensor.matmul(by_batch(A.ps[0][0:4, :], BB), ones[:, 0:4],
                             adjT_sb[:, :].unsqueeze(1).to_broadcast([P, BB, P]), start=True, stop=True)
            nc.tensor.matmul(A.ps[1][:, 0:2], WT_sb[:, :], a_sb[:, :], start=True, stop=True).then_inc(prep_mm, 1)
            walk(pe, pe_item, lambda pe: pe.wait_ge(prep_step, PREP_STEPS), lambda pe: pe.wait_ge(weights_split, 2))


def kernel(**inputs):
    import numpy as np
    import concourse.bacc as bacc
    from concourse.bass_utils import run_bass_kernel_spmd

    def get(name):
        return np.asarray(inputs[name])

    nc = bacc.Bacc("TRN2", target_bir_lowering=False, num_devices=1)
    laid = {
        "x": get("x"),
        "adj": get("adj"), "adjT": get("adj").T,
        "Wg0": get("L0_gnn_Wg0"), "bg0": get("L0_gnn_bg0"),
        "Wg1": get("L0_gnn_Wg1"), "bg1": get("L0_gnn_bg1"),
        "WihT": get("L0_gnn_Wih").transpose(2, 0, 1).reshape(P, -1),
        "WhhT": get("L0_gnn_Whh").transpose(2, 0, 1).reshape(P, -1),
        "bih": get("L0_gnn_bih").reshape(-1, P).T,
        "bhh": get("L0_gnn_bhh").reshape(-1, P).T,
        "W": get("L1_gnn_W"), "WT": get("L1_gnn_W").T,
        "a": get("L1_gnn_a").reshape(2, P).T,
    }
    arrays, args = {}, []
    for name, v in laid.items():
        v = np.ascontiguousarray(v)
        arrays["in_" + name] = v
        args.append(nc.dram_tensor("in_" + name, v.shape, mybir.dt.from_np(v.dtype), kind="ExternalInput").ap())
    args.append(nc.dram_tensor("out_x", (BATCHES, P, P), fp32, kind="ExternalOutput").ap())
    build(nc, *args)
    r = run_bass_kernel_spmd(nc, [arrays], core_ids=[0])
    return r.results[0]["out_x"]
```

```python
import concourse.bass as bass
from concourse import mybir
from contextlib import ExitStack

fp32 = mybir.dt.float32
fp32r = mybir.dt.float32r
bf16 = mybir.dt.bfloat16
ALU = mybir.AluOpType
ACT = mybir.ActivationFunctionType
AX = mybir.AxisListType

P = 128
BATCHES = 128
EPS = 1e-5
ALPHA = 0.2
MASKED = -(2.0 ** 100)

STREAMS = 2
GB = 8
ROUNDS = BATCHES // (STREAMS * GB)
COLS = GB * P
BANK = 512
NBANK = 4
BB = BANK // P
GATES = 4
I, F, G, O = range(GATES)
MAX_SKIP = 4

STEPS = [(1, 0, 0), (1, 0, 1)] + [(p, k, None) for p in range(2, MAX_SKIP + 1) for k in range(p)]
NSTEP = len(STEPS)
FORGETS = [sum(STEPS[s][1] > 0 for s in range(n + 1)) for n in range(NSTEP)]
NFORGET = FORGETS[-1]
S1, S2 = 0, 1
WH = slice(2, 2 + P)
ONE = 2 + P
WX = P + 3
TRIPLES = [(0, 3), (3, 6), (6, 8)]


def gates_of(step):
    return (I, G, O) if STEPS[step][1] == 0 else (F, I, G, O)


def width_of(step):
    p, _, half = STEPS[step]
    return GB // 2 * P if half is not None else GB * (P // p)


SEQ = """U.0 U.1 m.0 H.0 H.1 m.1 M.0 M.1 m.2 m.3 m.4 R.0 R.1 g.0 q.0 t.0 g.1 m.5 q.1 m.6 t.1 g.2 q.2 x.3 t.2
m.7 g.3 q.3 V.0 t.3 V.1 g.4 q.4 W.0 W.1 t.4 W.2 x.5 g.5 q.5 S.0 add.0 S.1 add.1 t.5 n.0 n.1 x.6 g.6
q.6 t.6 leaky.0 leaky.1 g.7 q.7 t.7 x.8 exp.0 exp.1 g.8 q.8 n.2 n.3 t.8 PT.0 PT.1 n.4 x.9 g.9 q.9
out.0 t.9 n.5 n.6 x.10 g.10 q.10 out.1 out.2 t.10 n.7 store T.0 T.1""".split()
LOW_BY_GPSIMD = (0, 6)
LSTM, ATT, NEXT = range(3)


def split(item):
    kind, _, number = item.partition(".")
    return kind, int(number) if number else 0


def part_of(item):
    kind = split(item)[0]
    if kind == "n":
        return NEXT
    return ATT if kind in ("m", "V", "W", "S", "add", "leaky", "exp", "PT", "out", "store") else LSTM


class Block:

    def __init__(self, item, j, part, engine, number, emptied, bank):
        self.item, self.j, self.part, self.engine = item, j, part, engine
        self.number, self.emptied, self.bank = number, emptied, bank


def gates_in(item):
    kind, step = split(item)
    n = len(gates_of(step))
    return range(2) if kind == "g" else range(2, n)


def plan_blocks():
    emptier = {"U": "act", "H": "act", "M": "dve", "R": "dve", "T": "dve", "V": "act", "W": "act", "S": "dve",
               "PT": "act", "out": "dve"}
    plan, held = [], None
    for item in SEQ:
        kind, number = split(item)
        if kind in emptier:
            name, members, engine = item, [number], emptier[kind]
        elif kind == "x":
            name, members, engine = f"g.{number}", range(len(gates_of(number))), "act"
        elif kind in "gq" and STEPS[number][1] == 0:
            name, members, engine = f"g.{number}", gates_in(item), "act"
        else:
            held = None if kind == "q" else held
            continue
        assert held is None, "a step's banks are full until its gates are done"
        held = item if kind == "x" else None
        for j in members:
            part = part_of(item)
            mine = [b for b in plan if b.part == part]
            plan.append(Block(name, j, part, engine, len(mine), sum(b.engine == engine for b in mine) + 1,
                              len(plan) % NBANK))
    return plan


PLAN = plan_blocks()


def blocks(item):
    return [b for b in PLAN if b.item == item]


def total(part, engine=None):
    return sum(b.part == part and engine in (None, b.engine) for b in PLAN)


AHEAD = 36
TURNS = ("BBABBBBBBAAABBAAABBAAABBAABAAABABAABBABABABBBBBABABBBBABAABBBAAABBABABBBBAAABBBAAABABBAAABBAAABBABBA"
         "AABBBBABBABABBABBABAABBABAAAAAABABAAAABABBAAABBAAABBBAAAAAABBBBAAAAB")


def merge(turns, A, B):
    steps = {"A": iter(A), "B": iter(B)}
    return [(stream, *next(steps[stream])) for stream in turns]


def taken(parts, items, r):
    return [(item, r) for item in items if part_of(item) in parts]


ORDER = merge(TURNS, taken({LSTM, ATT, NEXT}, SEQ, 0),
              taken({LSTM, ATT, NEXT}, SEQ[AHEAD:], 0) + taken({LSTM, ATT, NEXT}, SEQ[:AHEAD], 1))

FIRST_NORM = [(f"n.{k}", -1) for k in range(8)]
START_STEPS = {"A": FIRST_NORM + taken({LSTM, NEXT}, SEQ, 0),
               "B": FIRST_NORM + taken({LSTM, NEXT}, SEQ, 0) + taken({LSTM, ATT, NEXT}, SEQ[:AHEAD], 1)}
START_TURNS = ("BBBBBBBBBBBBABBAABBBABAABBBBBBBBAABBAABABBBABBBBBBABABBABAAAABABABABBBABABBAABBBABABBBBABBBAABABABAA"
               "BBAAABBBBABBABBBBABABBBBABABABBAAAAAAABBBBABAABBBAAAABBAAABABBAABB")
START = merge(START_TURNS, START_STEPS["A"], START_STEPS["B"])

END_STEPS = {"A": taken({LSTM, ATT}, SEQ, -1) + taken({ATT}, SEQ, 0),
             "B": taken({LSTM, ATT}, SEQ[AHEAD:], -1) + taken({ATT}, SEQ, 0)}
END_TURNS = ("BBAABBBBBBBAAAAAAABABBAABABAABAAABBABAABBBBBAAABABBBAABBBAABBAABBBBBAABAAAAABAAAAAAAAAABABABABAAAAAB"
             "ABBAABAABAAAAAAAAAABBAAAAAAABBAABBBABBBBABBBBAAAABAABAAAAAAAABAAABAAAA")
END = merge(END_TURNS, END_STEPS["A"], END_STEPS["B"])


def build(nc, x, adj, adjT, Wg0, bg0, Wg1, bg1, WihT, WhhT, bih, bhh, W, WT, a, out):
    ctx = ExitStack()
    with ctx:
        def sb(name, shape, dt=fp32):
            return ctx.enter_context(nc.sbuf_tensor(name, shape, dt))

        def sem(name):
            return ctx.enter_context(nc.semaphore(name))

        def half(ap, j):
            return ap[:, j * BANK:(j + 1) * BANK]

        W_x_hi, W_x_lo, W_h_hi, W_h_lo = (sb(n, [P, MAX_SKIP * GATES * P], fp32r)
                                          for n in ("W_x_hi", "W_x_lo", "W_h_hi", "W_h_lo"))
        adjT_sb = sb("adjT_sb", [P, P])
        adj_sb = sb("adj_sb", [P, P])
        Wg0_sb = sb("Wg0_sb", [P, P])
        Wg1_sb = sb("Wg1_sb", [P, P])
        bg1_bc = sb("bg1_bc", [P, P])
        bias_ih = sb("bias_ih", [P, MAX_SKIP * GATES])
        bias_hh = sb("bias_hh", [P, MAX_SKIP * GATES])
        bias = sb("bias", [P, MAX_SKIP * GATES])
        ones = sb("ones", [P, P])
        ident = sb("ident", [P, P])
        ident16 = sb("ident16", [P, P], bf16)
        mask16 = sb("mask16", [P, P], bf16)
        W_ext = sb("W_ext", [P, ONE])
        WT_sb = sb("WT_sb", [P, P])
        a_sb = sb("a_sb", [P, 2])
        neg_half = sb("neg_half", [P, GB])
        pick_hi = sb("pick_hi", [4, 2])
        pick_lo = sb("pick_lo", [4, 2])
        b0_raw = sb("b0_raw", [4, P])
        b0_parts = sb("b0_parts", [4, 2 * P], fp32r)
        b0_rows = sb("b0_rows", [4, P], fp32r)
        r_raw = sb("r_raw", [4, BANK])
        r_parts = sb("r_parts", [4, 2 * BANK], fp32r)
        r_rows = sb("r_rows", [4, BANK], fp32r)
        tmp_rows = sb("tmp_rows", [4, BANK])

        class Norm:
            pass

        class Stream:
            pass

        streams = []
        for s in range(STREAMS):
            S = Stream()
            S.s = s
            c = "ab"[s]
            S.x_res = sb("x_res_" + c, [P, COLS])
            S.xm = sb("xm_" + c, [P, COLS])
            S.xo = sb("xo_" + c, [P, COLS])
            S.hn = sb("hn_" + c, [P, COLS])
            S.h1 = S.hn
            S.U = sb("U_" + c, [P, COLS])
            S.m1 = S.U
            S.h_hi = sb("h_hi_" + c, [P, COLS], fp32r)
            S.h_lo = sb("h_lo_" + c, [P, COLS], fp32r)
            S.H = sb("H_" + c, [P, COLS])
            S.gate = [sb(f"gates{j}_" + c, [P, GATES, BANK]) for j in range(2)]
            S.cell = [sb(f"cell{j}_" + c, [P, BANK]) for j in range(2)]
            S.t_hi = sb("t_hi_" + c, [P, BANK], fp32r)
            S.t_lo = sb("t_lo_" + c, [P, BANK], fp32r)
            S.hn2 = sb("hn2_" + c, [P, COLS])
            S.prob = S.hn2
            S.hT = sb("hT_" + c, [P, COLS])
            S.PT = S.hT
            S.WhX = sb("WhX_" + c, [P, GB, WX])
            S.top = sb("top_" + c, [P, GB])
            S.top2 = sb("top2_" + c, [P, GB])
            S.rsum = sb("rsum_" + c, [P, GB])
            S.ps = [ctx.enter_context(nc.psum_tensor(f"ps{j}_" + c, [P, BANK], fp32)) for j in range(NBANK)]
            S.norm = []
            for n, y in enumerate((S.hn, S.hn2)):
                N = Norm()
                N.x = sb(f"x_norm_{c}", [P, COLS]) if n == 0 else S.xm
                N.y = y
                N.stats = sb(f"stats{n}_" + c, [P, GB, 6])
                N.mv = sb(f"mv{n}_" + c, [P, GB, 2])
                N.var = sb(f"var{n}_" + c, [P, GB])
                N.rstd = sb(f"rstd{n}_" + c, [P, GB])
                N.moments_ready = sem(f"moments{n}_ready_" + c)
                N.var_ready = sem(f"var{n}_ready_" + c)
                N.rstd_ready = sem(f"rstd{n}_ready_" + c)
                N.centred = sem(f"centred{n}_" + c)
                N.done = sem(f"norm{n}_done_" + c)
                S.norm.append(N)
            S.x_norm_in = sem("x_norm_in_" + c)
            S.x_res_in = sem("x_res_in_" + c)
            S.x_out = sem("x_out_" + c)
            S.filled = [sem("lstm_filled_" + c), sem("att_filled_" + c)]
            S.emptied = {"act": [sem("lstm_emptied_act_" + c), sem("att_emptied_act_" + c)],
                         "dve": [sem("lstm_emptied_dve_" + c), sem("att_emptied_dve_" + c)]}
            S.h2_hi_ready = sem("h2_hi_ready_" + c)
            S.input_ready = sem("input_ready_" + c)
            S.forget_ready = sem("forget_ready_" + c)
            S.cell_ready = sem("cell_ready_" + c)
            S.tanh_ready = sem("tanh_ready_" + c)
            S.h_whole = sem("h_whole_" + c)
            S.h_hi_ready = sem("h_hi_ready_" + c)
            S.h_split = sem("h_split_" + c)
            S.top_ready = sem("top_ready_" + c)
            S.leaky_ready = sem("leaky_ready_" + c)
            S.scores_ready = sem("scores_ready_" + c)
            S.exp_ready = sem("exp_ready_" + c)
            S.inverse_ready = sem("inverse_ready_" + c)
            streams.append(S)
        A, B = streams

        consts_in = sem("consts_in")
        CONSTS = 11 * 16
        RAW = [(0, 1), (0, 2), (1, 2), (0, 3), (1, 3), (0, 4), (1, 4)]
        places = [half(buf, j) for buf in (A.hn2, A.hT, A.xo, B.xo) for j in range(2)]
        raw = dict(zip(RAW, places))
        SPLIT_BEFORE = {'H.0': 1, 'R.0': 2, 'g.2': 3, 'g.4': 4}
        SPLIT_NEEDED = {f"{kind}.{s}": p for kind, s, p in (("g", 0, 1), ("g", 2, 2), ("g", 4, 3), ("g", 7, 4))}
        weights_in = {key: sem(f"weights_in{key[0]}{key[1]}") for key in RAW}
        fills = sem("fills")
        FILLS = 6
        diag_ready = sem("diag_ready")
        prep_mm = sem("prep_mm")
        prep_step = sem("prep_step")
        PREP_STEPS = 14
        weights_hi = sem("weights_hi")
        weights_split = sem("weights_split")

        def by_batch(ap, b=GB):
            return ap.rearrange("p (b c) -> p b c", b=b)

        def windows(buf, step):
            p, k, part = STEPS[step]
            if part is not None:
                return half(buf, part)
            nw = P // p
            v = by_batch(buf[:, :])[:, :, 0:nw * p].rearrange("q b (w p) -> q b w p", p=p)
            return v[:, :, :, k]

        def tile(ap, step):
            n = width_of(step)
            if STEPS[step][2] is not None:
                return ap[:, 0:n]
            return ap[:, 0:n].rearrange("p (b w) -> p b w", b=GB)

        def scratch(step):
            return step % 2 if STEPS[step][0] == 1 else 0

        def filled(q, block):
            return q * total(block.part) + block.number + 1

        def emptied(q, block):
            return 1 + q * total(block.part, block.engine) + block.emptied

        def wait_filled(eng, S, q, block):
            eng.wait_ge(S.filled[block.part], filled(q, block))

        def wait_emptied(eng, S, q, block):
            eng.wait_ge(S.emptied[block.engine][block.part], emptied(q, block))

        def take(pe, S, r, parts, block):
            n = PLAN.index(block)
            for other in PLAN[n - NBANK::-NBANK] if n >= NBANK else []:
                if other.part in parts:
                    wait_emptied(pe, S, r - (other.part == ATT), other)
                    return
            for engine in ("act", "dve"):
                pe.wait_ge(S.emptied[engine][LSTM], 1 + r * total(LSTM, engine))
                if ATT in parts:
                    pe.wait_ge(S.emptied[engine][ATT], 1 + (r - 1) * total(ATT, engine))

        def pe_item(pe, S, r, item, parts):
            mm = nc.tensor.matmul
            kind, k = split(item)
            mine = blocks(item)
            part = part_of(item)
            q = r - 1 if part == ATT else r

            def by_four(block, lhs, rhs):
                take(pe, S, r, parts, block)
                for b in range(BB):
                    c = (block.j * BB + b) * P
                    last = mm(S.ps[block.bank][:, b * P:(b + 1) * P], lhs[:, c:c + P], rhs[:, :],
                              start=(b == 0), stop=True, skip_group_check=True)
                last.then_inc(S.filled[part], 1)

            def transposed(block, src, j):
                take(pe, S, r, parts, block)
                for b in range(BB):
                    c = (j * BB + b) * P
                    last = nc.tensor.transpose(S.ps[block.bank][:, b * P:(b + 1) * P], src[:, c:c + P], ident[:, :])
                last.then_inc(S.filled[part], 1)

            if kind == "U":
                if k == 0:
                    pe.wait_ge(S.norm[0].done, r + 1)
                by_four(mine[0], S.hn, adjT_sb)
            elif kind == "H":
                take(pe, S, r, parts, mine[0])
                wait_emptied(pe, S, r, blocks(f"U.{k}")[0])
                ps = S.ps[mine[0].bank][:, :]
                mm(ps, Wg0_sb[:, :], half(S.U, k), start=True, stop=False)
                mm(ps, b0_rows[:, :], r_rows[:, :], start=False, stop=True).then_inc(S.filled[part], 1)
            elif kind == "M":
                wait_emptied(pe, S, r, blocks(f"H.{k}")[0])
                by_four(mine[0], S.h1, Wg1_sb)
            elif kind == "R":
                wait_emptied(pe, S, r, blocks(f"M.{k}")[0])
                by_four(mine[0], S.m1, adjT_sb)
            elif kind == "T":
                if k == 0:
                    pe.wait_ge(S.h_whole, (r + 1) * NSTEP)
                transposed(mine[0], S.H, k)
            elif kind == "x" or (kind in ("g", "q") and STEPS[k][1] == 0):
                p, at, part_of_group = STEPS[k]
                x_hi, x_lo = windows(S.h_hi, k), windows(S.h_lo, k)
                for m in (range(len(gates_of(k))) if kind == "x" else gates_in(item)):
                    gate, block = gates_of(k)[m], blocks(f"g.{k}")[m]
                    take(pe, S, r, parts, block)
                    ps = tile(S.ps[block.bank], k)
                    c = ((p - 1) * GATES + gate) * P
                    if m == 0 and part_of_group is not None:
                        pe.wait_ge(S.h2_hi_ready, r * 2 + part_of_group + 1)
                    elif m == 0 and at == 0:
                        pe.wait_ge(S.h_hi_ready, r * (NSTEP - 1) + k)
                    mm(ps, W_x_hi[:, c:c + P], x_hi, start=True, stop=False)
                    mm(ps, W_x_lo[:, c:c + P], x_hi, start=False, stop=False)
                    if m == 0 and part_of_group is not None:
                        wait_emptied(pe, S, r, blocks(f"R.{part_of_group}")[0])
                    elif m == 0 and at == 0:
                        pe.wait_ge(S.h_split, r * (NSTEP - 1) + k)
                    last = mm(ps, W_x_hi[:, c:c + P], x_lo, start=False, stop=(at == 0))
                    if at == 0:
                        last.then_inc(S.filled[part], 1)
            elif kind in ("g", "q"):
                p = STEPS[k][0]
                h_hi, h_lo = tile(S.t_hi, k), tile(S.t_lo, k)
                if kind == "g":
                    pe.wait_ge(S.h_hi_ready, r * (NSTEP - 1) + k)
                for m in gates_in(item):
                    gate, block = gates_of(k)[m], blocks(f"g.{k}")[m]
                    ps = tile(S.ps[block.bank], k)
                    c = ((p - 1) * GATES + gate) * P
                    mm(ps, W_h_hi[:, c:c + P], h_hi, start=False, stop=False)
                    mm(ps, W_h_lo[:, c:c + P], h_hi, start=False, stop=False)
                    if m == 0:
                        pe.wait_ge(S.h_split, r * (NSTEP - 1) + k)
                    mm(ps, W_h_hi[:, c:c + P], h_lo, start=False, stop=True).then_inc(S.filled[part], 1)
            elif kind == "V":
                if k == 0:
                    pe.wait_ge(S.norm[1].done, q + 1)
                transposed(mine[0], S.hn2, k)
            elif kind == "W":
                lo, hi = TRIPLES[k]
                wait_emptied(pe, S, q, blocks("V.1" if hi > BB else "V.0")[0])
                take(pe, S, r, parts, mine[0])
                for b in range(lo, hi):
                    last = mm(S.ps[mine[0].bank][:, (b - lo) * ONE:(b - lo + 1) * ONE], S.hT[:, b * P:(b + 1) * P],
                              W_ext[:, :], start=(b == lo), stop=True, skip_group_check=True)
                last.then_inc(S.filled[part], 1)
            elif kind == "S":
                wait_emptied(pe, S, q, blocks(f"W.{k + 1}")[0])
                take(pe, S, r, parts, mine[0])
                ps = by_batch(S.ps[mine[0].bank][:, :], BB)
                for b in range(BB):
                    s2 = S.WhX[:, k * BB + b, S2:S2 + 1]
                    mm(ps[:, b, :], s2.to_broadcast([P, P]), ident[:, :], start=(b == 0), stop=False,
                       is_transpose=True, skip_group_check=True)
                mm(ps, ident16[:, :], mask16[:, :].unsqueeze(1).to_broadcast([P, BB, P]), start=False, stop=True,
                   skip_group_check=True).then_inc(S.filled[part], 1)
            elif kind == "PT":
                pe.wait_ge(S.exp_ready, q * 2 + k + 1)
                transposed(mine[0], S.prob, k)
            elif kind == "out":
                lo, hi = TRIPLES[k]
                wait_emptied(pe, S, q, blocks("PT.1" if hi > BB else "PT.0")[0])
                take(pe, S, r, parts, mine[0])
                for b in range(lo, hi):
                    last = mm(S.ps[mine[0].bank][:, (b - lo) * (P + 1):(b - lo + 1) * (P + 1)],
                              S.PT[:, b * P:(b + 1) * P], S.WhX[:, b, WH.start:WX],
                              start=(b == lo), stop=True, skip_group_check=True)
                last.then_inc(S.filled[part], 1)

        def act_item(act, S, r, item, parts):
            kind, k = split(item)
            mine = blocks(item)
            part = part_of(item)
            q = r - 1 if part == ATT else r

            def empty(block, dst, func, **kw):
                wait_filled(act, S, q, block)
                nc.scalar.activation(dst, S.ps[block.bank][:, :], func, **kw).then_inc(S.emptied["act"][part], 1)

            if kind == "U":
                empty(mine[0], half(S.U, k), ACT.Copy)
            elif kind == "H":
                empty(mine[0], half(S.h1, k), ACT.Relu)
            elif kind == "R":
                wait_filled(act, S, q, mine[0])
                nc.scalar.activation(half(S.h_hi, k), S.ps[mine[0].bank][:, :], ACT.Relu).then_inc(S.h2_hi_ready, 1)
            elif kind in ("g", "q"):
                p, w = STEPS[k][0], width_of(k)
                for m in gates_in(item):
                    gate, block = gates_of(k)[m], blocks(f"g.{k}")[m]
                    wait_filled(act, S, q, block)
                    c = (p - 1) * GATES + gate
                    nc.scalar.activation(S.gate[scratch(k)][:, gate, 0:w], S.ps[block.bank][:, 0:w],
                                         ACT.Tanh if gate == G else ACT.Sigmoid,
                                         bias=bias[:, c:c + 1]).then_inc(S.emptied["act"][part], 1)
            elif kind == "t":
                w = width_of(k)
                act.wait_ge(S.cell_ready, r * NSTEP + k + 1)
                nc.scalar.activation(S.gate[scratch(k)][:, G, 0:w], S.cell[scratch(k)][:, 0:w], ACT.Tanh)\
                    .then_inc(S.tanh_ready, 1)
            elif kind == "V":
                empty(mine[0], half(S.hT, k), ACT.Copy)
            elif kind == "PT":
                empty(mine[0], half(S.PT, k), ACT.Copy)
            elif kind == "W":
                lo, hi = TRIPLES[k]
                wait_filled(act, S, q, mine[0])
                src = S.ps[mine[0].bank][:, 0:(hi - lo) * ONE].rearrange("p (b c) -> p b c", c=ONE)
                nc.scalar.activation(S.WhX[:, lo:hi, 0:ONE], src, ACT.Copy).then_inc(S.emptied["act"][part], 1)
            elif kind == "exp":
                act.wait_ge(S.scores_ready, q * 2 + k + 1)
                nc.scalar.activation(half(S.prob, k), half(S.prob, k), ACT.Exp).then_inc(S.exp_ready, 1)
            elif kind == "store":
                act.wait_ge(S.emptied["dve"][ATT], 1 + (q + 1) * total(ATT, "dve"))
                act.dma_start(out_v[:, group(S, q), :], by_batch(S.xo[:, :])).then_inc(S.x_out, 16)

        x_v = x.rearrange("b t d -> t b d")
        out_v = out.rearrange("b t d -> t b d")

        def group(S, g):
            return bass.ds((g * STREAMS + S.s) * GB, GB)

        def vector_centres(S, N, g):
            return isinstance(g, int) and g == (0 if N is S.norm[0] else ROUNDS - 1)

        def low_part(eng, unit, S, r, k):
            final = STEPS[k][1] == STEPS[k][0] - 1
            output = tile(S.gate[scratch(k)][:, O, :], k)
            whole, hi, lo = ((windows(S.H, k), windows(S.h_hi, k), windows(S.h_lo, k)) if final else
                             (output, tile(S.t_hi, k), tile(S.t_lo, k)))
            eng.wait_ge(S.h_hi_ready, r * (NSTEP - 1) + k + 1)
            unit.tensor_tensor(lo, whole, hi.bitcast(fp32), ALU.subtract).then_inc(S.h_split, 1)

        def dve_norm(dve, S, N, g, piece):
            if piece < 4:
                if piece == 0 and N is S.norm[0]:
                    dve.wait_ge(S.x_norm_in, (g + 1) * 16)
                elif piece == 0:
                    dve.wait_ge(S.emptied["dve"][LSTM], 1 + (g + 1) * total(LSTM, "dve"))
                for b in range(2 * piece, 2 * piece + 2):
                    nc.vector.bn_stats(N.stats[:, b, :], N.x[:, b * P:(b + 1) * P])
                if piece == 3:
                    dve.drain()
                    for b in range(GB):
                        last = nc.vector.bn_aggr(N.mv[:, b, :], N.stats[:, b, :])
                    last.then_inc(N.moments_ready, 1)
            elif piece == 4:
                dve.wait_ge(N.moments_ready, g + 1)
                nc.vector.tensor_scalar(N.var[:, :], N.mv[:, :, 1], EPS, None, ALU.add).then_inc(N.var_ready, 1)
            elif piece in (5, 6) and vector_centres(S, N, g):
                j = piece - 5
                for b in range(j * BB, (j + 1) * BB):
                    c = slice(b * P, (b + 1) * P)
                    last = nc.vector.tensor_scalar(N.y[:, c], N.x[:, c], N.mv[:, b, 0:1], None, ALU.subtract)
                last.then_inc(N.centred, 1)
            elif piece == 7:
                dve.wait_ge(N.centred, 2 * (g + 1))
                dve.wait_ge(N.rstd_ready, g + 1)
                nc.vector.scalar_tensor_tensor(by_batch(N.y[:, :]), by_batch(N.y[:, :]), 0.0,
                                               N.rstd[:, :].unsqueeze(2).to_broadcast([P, GB, P]),
                                               ALU.max, ALU.mult).then_inc(N.done, 1)

        def dve_item(dve, S, r, item, parts):
            kind, k = split(item)
            mine = blocks(item)
            part = part_of(item)
            q = r - 1 if part == ATT else r
            if kind == "n":
                dve_norm(dve, S, S.norm[0], r + 1, k)
            elif kind == "m":
                dve_norm(dve, S, S.norm[1], q, k)
            elif kind == "M":
                wait_filled(dve, S, q, mine[0])
                nc.vector.tensor_tensor(by_batch(half(S.m1, k), BB), by_batch(S.ps[mine[0].bank][:, :], BB),
                                        bg1_bc[:, :].unsqueeze(1).to_broadcast([P, BB, P]), ALU.add)\
                    .then_inc(S.emptied["dve"][part], 1)
            elif kind == "R":
                dve.wait_ge(S.h2_hi_ready, r * 2 + k + 1)
                nc.vector.scalar_tensor_tensor(half(S.h_lo, k), S.ps[mine[0].bank][:, :], 0.0,
                                               half(S.h_hi, k).bitcast(fp32), ALU.max, ALU.subtract)\
                    .then_inc(S.emptied["dve"][part], 1)
            elif kind == "T":
                if k == 0:
                    dve.wait_ge(S.x_res_in, (r + 1) * 16)
                wait_filled(dve, S, q, mine[0])
                nc.vector.tensor_tensor(half(S.xm, k), half(S.x_res, k), S.ps[mine[0].bank][:, :],
                                        ALU.add).then_inc(S.emptied["dve"][part], 1)
            elif kind == "q":
                w = width_of(k)
                gate, cell = S.gate[scratch(k)], S.cell[scratch(k)]
                wait_emptied(dve, S, q, blocks(f"g.{k}")[gates_of(k).index(G)])
                if STEPS[k][1] == 0:
                    nc.vector.tensor_tensor(cell[:, 0:w], gate[:, I, 0:w], gate[:, G, 0:w], ALU.mult)\
                        .then_inc(S.cell_ready, 1)
                else:
                    nc.vector.tensor_tensor(gate[:, I, 0:w], gate[:, I, 0:w], gate[:, G, 0:w], ALU.mult)\
                        .then_inc(S.input_ready, 1)
                    dve.wait_ge(S.input_ready, r * NFORGET + FORGETS[k])
                    dve.wait_ge(S.forget_ready, r * NFORGET + FORGETS[k])
                    nc.vector.tensor_tensor(cell[:, 0:w], gate[:, I, 0:w], gate[:, F, 0:w], ALU.add)\
                        .then_inc(S.cell_ready, 1)
            elif kind == "t":
                gate = S.gate[scratch(k)]
                final = STEPS[k][1] == STEPS[k][0] - 1
                dve.wait_ge(S.tanh_ready, r * NSTEP + k + 1)
                o, t = tile(gate[:, O, :], k), tile(gate[:, G, :], k)
                whole = windows(S.H, k) if final else o
                nc.vector.tensor_tensor(whole, o, t, ALU.mult).then_inc(S.h_whole, 1)
                if k == NSTEP - 1:
                    return
                hi = windows(S.h_hi, k) if final else tile(S.t_hi, k)
                dve.wait_ge(S.h_whole, r * NSTEP + k + 1)
                nc.vector.tensor_copy(hi, whole).then_inc(S.h_hi_ready, 1)
                if k not in LOW_BY_GPSIMD:
                    low_part(dve, nc.vector, S, r, k)
            elif kind == "S":
                wait_filled(dve, S, q, mine[0])
                last = nc.vector.reduce_max(S.top[:, k * BB:(k + 1) * BB], by_batch(S.ps[mine[0].bank][:, :], BB), AX.X)
                if k == 1:
                    last.then_inc(S.top_ready, 1)
                    dve.wait_ge(S.top_ready, q * 3 + 1)
                    wait_emptied(dve, S, q, blocks("W.2")[0])
                    nc.vector.tensor_tensor(S.top[:, :], S.top[:, :], S.WhX[:, :, S1], ALU.add)\
                        .then_inc(S.top_ready, 1)
                    dve.wait_ge(S.top_ready, q * 3 + 2)
                    nc.vector.scalar_tensor_tensor(S.top2[:, :], S.top[:, :], ALPHA, S.top[:, :], ALU.mult, ALU.max)\
                        .then_inc(S.top_ready, 1)
            elif kind == "add":
                block = blocks(f"S.{k}")[0]
                if k == 0:
                    wait_emptied(dve, S, q, blocks("W.1")[0])
                nc.vector.tensor_tensor(by_batch(half(S.prob, k), BB), by_batch(S.ps[block.bank][:, :], BB),
                                        S.WhX[:, k * BB:(k + 1) * BB, S1:S1 + 1].to_broadcast([P, BB, P]), ALU.add)\
                    .then_inc(S.emptied["dve"][part], 1)
            elif kind == "leaky":
                wait_emptied(dve, S, q, blocks(f"S.{k}")[0])
                s = half(S.prob, k)
                nc.vector.scalar_tensor_tensor(s, s, ALPHA, s, ALU.mult, ALU.max).then_inc(S.leaky_ready, 1)
            elif kind == "out":
                lo, hi = TRIPLES[k]
                wait_filled(dve, S, q, mine[0])
                src = S.ps[mine[0].bank][:, 0:(hi - lo) * (P + 1)].rearrange("p (b c) -> p b c", c=P + 1)
                nc.vector.reciprocal(S.rsum[:, lo:hi], src[:, :, P]).then_inc(S.inverse_ready, 1)
                if k == 0:
                    dve.wait_ge(S.x_out, 1 + q * 16)
                dve.wait_ge(S.inverse_ready, q * 3 + k + 1)
                for b in range(lo, hi):
                    c = slice(b * P, (b + 1) * P)
                    last = nc.vector.scalar_tensor_tensor(S.xo[:, c], src[:, b - lo, 0:P], S.rsum[:, b:b + 1],
                                                          S.xm[:, c], ALU.mult, ALU.add)
                last.then_inc(S.emptied["dve"][part], 1)

        def pool_norm(pool, S, N, g, piece):
            if piece == 4:
                pool.wait_ge(N.var_ready, g + 1)
                nc.gpsimd.tensor_tensor(N.rstd[:, :], N.var[:, :], neg_half[:, :], ALU.pow).then_inc(N.rstd_ready, 1)
            elif piece in (5, 6) and not vector_centres(S, N, g):
                if piece == 5:
                    pool.wait_ge(N.moments_ready, g + 1)
                j = piece - 5
                nc.gpsimd.tensor_tensor(by_batch(half(N.y, j), BB), by_batch(half(N.x, j), BB),
                                        N.mv[:, j * BB:(j + 1) * BB, 0:1].to_broadcast([P, BB, P]), ALU.subtract)\
                    .then_inc(N.centred, 1)

        def pool_item(pool, S, r, item, parts):
            kind, k = split(item)
            part = part_of(item)
            q = r - 1 if part == ATT else r
            if kind == "n":
                pool_norm(pool, S, S.norm[0], r + 1, k)
            elif kind == "m":
                pool_norm(pool, S, S.norm[1], q, k)
            elif kind == "g" and STEPS[k][1] > 0:
                w = width_of(k)
                forget = S.gate[scratch(k)][:, F, 0:w]
                wait_emptied(pool, S, q, blocks(item)[gates_of(k).index(F)])
                nc.gpsimd.tensor_tensor(forget, forget, S.cell[scratch(k)][:, 0:w], ALU.mult)\
                    .then_inc(S.forget_ready, 1)
            elif kind == "t" and k in LOW_BY_GPSIMD:
                low_part(pool, nc.gpsimd, S, r, k)
            elif kind == "leaky":
                pool.wait_ge(S.leaky_ready, q * 2 + k + 1)
                if k == 0:
                    pool.wait_ge(S.top_ready, q * 3 + 3)
                s = by_batch(half(S.prob, k), BB)
                nc.gpsimd.tensor_tensor(s, s, S.top2[:, k * BB:(k + 1) * BB].unsqueeze(2).to_broadcast([P, BB, P]),
                                        ALU.subtract).then_inc(S.scores_ready, 1)

        def walk(eng, do, preparation):
            def parts_of_round(r):
                if not isinstance(r, int):
                    return {LSTM, ATT, NEXT}
                return {p for p, g in ((LSTM, r), (ATT, r - 1), (NEXT, r + 1)) if 0 <= g < ROUNDS}

            def steps(order, base):
                for stream, item, r in order:
                    r = base + r
                    if stream == "B" and isinstance(r, int) and r == 0 and item in preparation:
                        preparation[item](eng)
                    do(eng, A if stream == "A" else B, r, item, parts_of_round(r))

            steps(START, 0)
            with eng.Fori(1, ROUNDS - 1) as r:
                steps(ORDER, r)
            steps(END, ROUNDS)

        block = ctx.enter_context(nc.Block())

        @block.sync
        def _(sp):
            def load_norm(S, g):
                if not (isinstance(g, int) and g == 0):
                    sp.wait_ge(S.norm[0].centred, g * 2)
                sp.dma_start(by_batch(S.norm[0].x[:, :]), x_v[:, group(S, g), :]).then_inc(S.x_norm_in, 16)

            def load_res(S, g):
                if not (isinstance(g, int) and g == 0):
                    sp.wait_ge(S.emptied["dve"][LSTM], 1 + g * total(LSTM, "dve"))
                sp.dma_start(by_batch(S.x_res[:, :]), x_v[:, group(S, g), :]).then_inc(S.x_res_in, 16)

            load_norm(B, 0)
            sp.dma_start(adjT_sb[:, :], adjT).then_inc(consts_in, 16)
            sp.dma_start(b0_raw[:, :], bg0.unsqueeze(0).to_broadcast([4, P])).then_inc(consts_in, 16)
            sp.dma_start(Wg0_sb[:, :], Wg0).then_inc(consts_in, 16)
            sp.dma_start(Wg1_sb[:, :], Wg1).then_inc(consts_in, 16)
            sp.dma_start(bg1_bc[:, :], bg1.unsqueeze(0).to_broadcast([P, P])).then_inc(consts_in, 16)
            sp.dma_start(bias_ih[:, :], bih).then_inc(consts_in, 16)
            sp.dma_start(bias_hh[:, :], bhh).then_inc(consts_in, 16)
            sp.dma_start(W_ext[:, WH], W).then_inc(consts_in, 16)
            sp.dma_start(WT_sb[:, :], WT).then_inc(consts_in, 16)
            sp.dma_start(a_sb[:, :], a).then_inc(consts_in, 16)
            sp.dma_start(adj_sb[:, :], adj).then_inc(consts_in, 16)
            for n, (which, p) in enumerate(RAW):
                source = (WihT, WhhT)[which]
                sp.dma_start(raw[which, p], half(source, p - 1)).then_inc(weights_in[which, p], 16)
                if n == 2:
                    load_norm(A, 0)
            for S in (B, A):
                load_res(S, 0)
            with sp.Fori(1, ROUNDS) as g:
                for S in (B, A):
                    load_norm(S, g)
                    load_res(S, g)
            for S in (B, A):
                sp.wait_ge(S.x_out, 1 + 16 * ROUNDS)

        @block.gpsimd
        def _(pool):
            pool.memset(neg_half[:, :], -0.5).then_inc(fills, 1)
            pool.memset(ones[:, :], 1.0).then_inc(fills, 1)
            pool.memset(ident[:, :], 0.0).then_inc(fills, 1)
            for S in (A, B):
                pool.memset(S.WhX[:, :, ONE:WX], 1.0).then_inc(fills, 1)
            pool.memset(pick_hi[:, :], 0.0).then_inc(fills, 1)
            pool.wait_ge(fills, FILLS)
            pool.affine_select(out=ident[:, :], in_=ident[:, :], compare_op=ALU.not_equal, fill=1.0, base=0,
                               pattern=[[-1, P]], channel_multiplier=1).then_inc(diag_ready, 1)
            pool.affine_select(out=pick_hi[:, 0:1], in_=pick_hi[:, 0:1], compare_op=ALU.is_ge, fill=1.0, base=-2,
                               pattern=[[0, 1]], channel_multiplier=1).then_inc(diag_ready, 1)
            for n, row in enumerate((0, 2)):
                pool.wait_ge(diag_ready, 2 + n)
                pool.affine_select(out=pick_hi[:, 1:2], in_=pick_hi[:, 1:2], compare_op=ALU.not_equal, fill=1.0,
                                   base=-row, pattern=[[0, 1]], channel_multiplier=1).then_inc(diag_ready, 1)
            walk(pool, pool_item, {})

        @block.scalar
        def _(act):
            act.wait_ge(fills, FILLS)
            for S in (A, B):
                nc.scalar.activation(S.rsum[:, 2:3], neg_half[:, 0:1], ACT.Copy).then_inc(S.x_out, 1)
                for part in (LSTM, ATT):
                    nc.scalar.activation(S.rsum[:, part:part + 1], neg_half[:, 0:1], ACT.Copy)\
                        .then_inc(S.emptied["act"][part], 1)

            def high_parts(act, p):
                for which, length in RAW:
                    if length == p:
                        act.wait_ge(weights_in[which, p], 16)
                        nc.scalar.activation(half((W_x_hi, W_h_hi)[which], p - 1), raw[which, p], ACT.Copy)\
                            .then_inc(weights_hi, 1)

            walk(act, act_item, {item: lambda act, p=p: high_parts(act, p) for item, p in SPLIT_BEFORE.items()})

        @block.vector
        def _(dve):
            links = [0]

            def link(ins):
                links[0] += 1
                ins.then_inc(prep_step, 1)
                dve.wait_ge(prep_step, links[0])

            dve.wait_ge(fills, FILLS)
            for S in (A, B):
                for part in (LSTM, ATT):
                    nc.vector.tensor_copy(S.top[:, part:part + 1], neg_half[:, 0:1])\
                        .then_inc(S.emptied["dve"][part], 1)

            def make_constants(dve):
                dve.wait_ge(consts_in, CONSTS)
                dve.wait_ge(diag_ready, 4)
                link(nc.vector.tensor_copy(ident16[:, :], ident[:, :]))
                link(nc.vector.tensor_scalar(mask16[:, :], adj_sb[:, :], 0.0, MASKED, ALU.is_equal, ALU.mult))
                link(nc.vector.tensor_tensor(bias[:, :], bias_ih[:, :], bias_hh[:, :], ALU.add))
                dve.wait_ge(prep_mm, 1)
                link(nc.vector.tensor_copy(r_raw[:, :], A.ps[0][0:4, :]))
                link(nc.vector.tensor_copy(W_ext[:, 0:2], A.ps[1][:, 0:2]))
                link(nc.vector.tensor_scalar(pick_lo[:, :], pick_hi[:, :], -1.0, 1.0, ALU.mult, ALU.add))
                for raw, parts, rows, c, w in ((b0_raw, b0_parts, b0_rows, 0, P), (r_raw, r_parts, r_rows, 1, BANK)):
                    link(nc.vector.tensor_copy(parts[:, 0:w], raw[:, :]))
                    link(nc.vector.tensor_tensor(parts[:, w:2 * w], raw[:, :], parts[:, 0:w].bitcast(fp32), ALU.subtract))
                    link(nc.vector.tensor_scalar(tmp_rows[:, 0:w], parts[:, 0:w].bitcast(fp32), pick_hi[:, c:c + 1], None,
                                                 ALU.mult))
                    link(nc.vector.scalar_tensor_tensor(rows[:, :], parts[:, w:2 * w].bitcast(fp32), pick_lo[:, c:c + 1],
                                                        tmp_rows[:, 0:w], ALU.mult, ALU.add))

            def low_parts(dve, p):
                for n, (which, length) in enumerate(RAW):
                    if length == p:
                        hi, lo = ((W_x_hi, W_x_lo), (W_h_hi, W_h_lo))[which]
                        dve.wait_ge(weights_hi, n + 1)
                        nc.vector.tensor_tensor(half(lo, p - 1), raw[which, p], half(hi, p - 1).bitcast(fp32),
                                                ALU.subtract).then_inc(weights_split, 1)

            walk(dve, dve_item, {"U.0": make_constants,
                                 **{item: lambda dve, p=p: low_parts(dve, p) for item, p in SPLIT_BEFORE.items()}})

        @block.tensor
        def _(pe):
            pe.wait_ge(consts_in, CONSTS)
            pe.wait_ge(fills, FILLS)
            nc.tensor.matmul(by_batch(A.ps[0][0:4, :], BB), ones[:, 0:4],
                             adjT_sb[:, :].unsqueeze(1).to_broadcast([P, BB, P]), start=True, stop=True)
            nc.tensor.matmul(A.ps[1][:, 0:2], WT_sb[:, :], a_sb[:, :], start=True, stop=True).then_inc(prep_mm, 1)
            walk(pe, pe_item, {"H.0": lambda pe: pe.wait_ge(prep_step, PREP_STEPS),
                               **{item: lambda pe, p=p: pe.wait_ge(weights_split, sum(length <= p for _, length in RAW))
                                  for item, p in SPLIT_NEEDED.items()}})


def kernel(**inputs):
    import numpy as np
    import concourse.bacc as bacc
    from concourse.bass_utils import run_bass_kernel_spmd

    def get(name):
        return np.asarray(inputs[name])

    nc = bacc.Bacc("TRN2", target_bir_lowering=False, num_devices=1)
    laid = {
        "x": get("x"),
        "adj": get("adj"), "adjT": get("adj").T,
        "Wg0": get("L0_gnn_Wg0"), "bg0": get("L0_gnn_bg0"),
        "Wg1": get("L0_gnn_Wg1"), "bg1": get("L0_gnn_bg1"),
        "WihT": get("L0_gnn_Wih").transpose(2, 0, 1).reshape(P, -1),
        "WhhT": get("L0_gnn_Whh").transpose(2, 0, 1).reshape(P, -1),
        "bih": get("L0_gnn_bih").reshape(-1, P).T,
        "bhh": get("L0_gnn_bhh").reshape(-1, P).T,
        "W": get("L1_gnn_W"), "WT": get("L1_gnn_W").T,
        "a": get("L1_gnn_a").reshape(2, P).T,
    }
    arrays, args = {}, []
    for name, v in laid.items():
        v = np.ascontiguousarray(v)
        arrays["in_" + name] = v
        args.append(nc.dram_tensor("in_" + name, v.shape, mybir.dt.from_np(v.dtype), kind="ExternalInput").ap())
    args.append(nc.dram_tensor("out_x", (BATCHES, P, P), fp32, kind="ExternalOutput").ap())
    build(nc, *args)
    r = run_bass_kernel_spmd(nc, [arrays], core_ids=[0])
    return r.results[0]["out_x"]
```
